# Optimizing a Trainium2 kernel written in Bass

```python
import numpy as np
import jax
import jax.numpy as jnp

def _softmax(x, axis=-1):
    return jax.nn.softmax(x, axis=axis)

def _gelu(x):
    return jax.nn.gelu(x, approximate=True)

def _silu(x):
    return jax.nn.silu(x)

def _sigmoid(x):
    return jax.nn.sigmoid(x)

def _layernorm(x, axis=-1, eps=1e-05):
    m = jnp.mean(x, axis=axis, keepdims=True)
    v = jnp.var(x, axis=axis, keepdims=True)
    return (x - m) / jnp.sqrt(v + eps)

def _scatter_add(tgt, idx, src, axis=0):
    return tgt.at[idx].add(src)

def _segment_sum(src, seg, n):
    return jax.ops.segment_sum(src, seg, n)
kernel_name = 'mk_dlrm_tower_d1_rec_r8_702ea5'

def setup_inputs(seed: int=0):
    np.random.seed(seed)
    _w = jnp.asarray

    def _rec_inputs():
        import jax
        import jax.numpy as jnp
        _tk = jax.random.key(seed)
        ids = jnp.stack([jax.random.randint(jax.random.fold_in(_tk, 200 + f), (2048,), 0, v, jnp.int32) for f, v in enumerate([1250, 12500, 1250, 125000, 1250, 1250, 1000, 1000, 12500, 1000, 1000, 1000, 1000, 1250, 12500, 1000, 1000, 12500, 12500, 1000, 12500, 1250, 1000, 1250, 1250, 12500])], axis=1)
        tbl_0 = 0.05 * jax.random.normal(jax.random.fold_in(_tk, 500 + 0), (1250, 128), jnp.float32)
        tbl_1 = 0.05 * jax.random.normal(jax.random.fold_in(_tk, 500 + 1), (12500, 128), jnp.float32)
        tbl_2 = 0.05 * jax.random.normal(jax.random.fold_in(_tk, 500 + 2), (1250, 128), jnp.float32)
        tbl_3 = 0.05 * jax.random.normal(jax.random.fold_in(_tk, 500 + 3), (125000, 128), jnp.float32)
        tbl_4 = 0.05 * jax.random.normal(jax.random.fold_in(_tk, 500 + 4), (1250, 128), jnp.float32)
        tbl_5 = 0.05 * jax.random.normal(jax.random.fold_in(_tk, 500 + 5), (1250, 128), jnp.float32)
        tbl_6 = 0.05 * jax.random.normal(jax.random.fold_in(_tk, 500 + 6), (1000, 128), jnp.float32)
        tbl_7 = 0.05 * jax.random.normal(jax.random.fold_in(_tk, 500 + 7), (1000, 128), jnp.float32)
        tbl_8 = 0.05 * jax.random.normal(jax.random.fold_in(_tk, 500 + 8), (12500, 128), jnp.float32)
        tbl_9 = 0.05 * jax.random.normal(jax.random.fold_in(_tk, 500 + 9), (1000, 128), jnp.float32)
        tbl_10 = 0.05 * jax.random.normal(jax.random.fold_in(_tk, 500 + 10), (1000, 128), jnp.float32)
        tbl_11 = 0.05 * jax.random.normal(jax.random.fold_in(_tk, 500 + 11), (1000, 128), jnp.float32)
        tbl_12 = 0.05 * jax.random.normal(jax.random.fold_in(_tk, 500 + 12), (1000, 128), jnp.float32)
        tbl_13 = 0.05 * jax.random.normal(jax.random.fold_in(_tk, 500 + 13), (1250, 128), jnp.float32)
        tbl_14 = 0.05 * jax.random.normal(jax.random.fold_in(_tk, 500 + 14), (12500, 128), jnp.float32)
        tbl_15 = 0.05 * jax.random.normal(jax.random.fold_in(_tk, 500 + 15), (1000, 128), jnp.float32)
        tbl_16 = 0.05 * jax.random.normal(jax.random.fold_in(_tk, 500 + 16), (1000, 128), jnp.float32)
        tbl_17 = 0.05 * jax.random.normal(jax.random.fold_in(_tk, 500 + 17), (12500, 128), jnp.float32)
        tbl_18 = 0.05 * jax.random.normal(jax.random.fold_in(_tk, 500 + 18), (12500, 128), jnp.float32)
        tbl_19 = 0.05 * jax.random.normal(jax.random.fold_in(_tk, 500 + 19), (1000, 128), jnp.float32)
        tbl_20 = 0.05 * jax.random.normal(jax.random.fold_in(_tk, 500 + 20), (12500, 128), jnp.float32)
        tbl_21 = 0.05 * jax.random.normal(jax.random.fold_in(_tk, 500 + 21), (1250, 128), jnp.float32)
        tbl_22 = 0.05 * jax.random.normal(jax.random.fold_in(_tk, 500 + 22), (1000, 128), jnp.float32)
        tbl_23 = 0.05 * jax.random.normal(jax.random.fold_in(_tk, 500 + 23), (1250, 128), jnp.float32)
        tbl_24 = 0.05 * jax.random.normal(jax.random.fold_in(_tk, 500 + 24), (1250, 128), jnp.float32)
        tbl_25 = 0.05 * jax.random.normal(jax.random.fold_in(_tk, 500 + 25), (12500, 128), jnp.float32)
        _rk = jax.random.fold_in(_tk, 7)
        r_dense_x = -0.000514642 + 1.00011 * jax.random.normal(jax.random.fold_in(_rk, 101), (2048, 128), jnp.float32)
        W_top1 = 0.0456912 * jax.random.normal(jax.random.fold_in(_tk, 801), (479, 512), jnp.float32)
        W_top2 = 0.0441942 * jax.random.normal(jax.random.fold_in(_tk, 802), (512, 256), jnp.float32)
        W_top3 = 0.0625 * jax.random.normal(jax.random.fold_in(_tk, 803), (256, 1), jnp.float32)
        b_top1 = jnp.zeros((512,), jnp.float32)
        b_top2 = jnp.zeros((256,), jnp.float32)
        return (r_dense_x, ids, tbl_0, tbl_1, tbl_2, tbl_3, tbl_4, tbl_5, tbl_6, tbl_7, tbl_8, tbl_9, tbl_10, tbl_11, tbl_12, tbl_13, tbl_14, tbl_15, tbl_16, tbl_17, tbl_18, tbl_19, tbl_20, tbl_21, tbl_22, tbl_23, tbl_24, tbl_25, W_top1, b_top1, W_top2, b_top2, W_top3)
    r_dense_x, ids, tbl_0, tbl_1, tbl_2, tbl_3, tbl_4, tbl_5, tbl_6, tbl_7, tbl_8, tbl_9, tbl_10, tbl_11, tbl_12, tbl_13, tbl_14, tbl_15, tbl_16, tbl_17, tbl_18, tbl_19, tbl_20, tbl_21, tbl_22, tbl_23, tbl_24, tbl_25, W_top1, b_top1, W_top2, b_top2, W_top3 = _rec_inputs()

    def _L0_rec_setup():
        import jax, jax.numpy as jnp
        import numpy as np
        F = 26
        D = 128
        B = 2048
        _TRIU_I, _TRIU_J = np.triu_indices(F + 1, k=1)
        _TRIU_I = jnp.asarray(_TRIU_I)
        _TRIU_J = jnp.asarray(_TRIU_J)
        key = jax.random.key(seed)
        k1, k2 = jax.random.split(key)
        sparse_x = jax.random.normal(k1, (B, F, D), dtype=jnp.float32)
        dense_x = jax.random.normal(k2, (B, D), dtype=jnp.float32)
        return {'sparse_x': sparse_x, 'dense_x': dense_x}
    _L0_rec_all = _L0_rec_setup()
    _L0_rec_in = {k: v for k, v in _L0_rec_all.items() if k in ()}
    del _L0_rec_all
    return {'r_dense_x': r_dense_x, 'ids': ids, 'tbl_0': tbl_0, 'tbl_1': tbl_1, 'tbl_2': tbl_2, 'tbl_3': tbl_3, 'tbl_4': tbl_4, 'tbl_5': tbl_5, 'tbl_6': tbl_6, 'tbl_7': tbl_7, 'tbl_8': tbl_8, 'tbl_9': tbl_9, 'tbl_10': tbl_10, 'tbl_11': tbl_11, 'tbl_12': tbl_12, 'tbl_13': tbl_13, 'tbl_14': tbl_14, 'tbl_15': tbl_15, 'tbl_16': tbl_16, 'tbl_17': tbl_17, 'tbl_18': tbl_18, 'tbl_19': tbl_19, 'tbl_20': tbl_20, 'tbl_21': tbl_21, 'tbl_22': tbl_22, 'tbl_23': tbl_23, 'tbl_24': tbl_24, 'tbl_25': tbl_25, 'W_top1': W_top1, 'b_top1': b_top1, 'W_top2': W_top2, 'b_top2': b_top2, 'W_top3': W_top3}

def reference(r_dense_x, ids, tbl_0, tbl_1, tbl_2, tbl_3, tbl_4, tbl_5, tbl_6, tbl_7, tbl_8, tbl_9, tbl_10, tbl_11, tbl_12, tbl_13, tbl_14, tbl_15, tbl_16, tbl_17, tbl_18, tbl_19, tbl_20, tbl_21, tbl_22, tbl_23, tbl_24, tbl_25, W_top1, b_top1, W_top2, b_top2, W_top3):
    import jax
    import jax.numpy as jnp

    def _L0_rec_ref(sparse_x, dense_x):
        import jax, jax.numpy as jnp
        import numpy as np
        F = 26
        D = 128
        B = 2048
        _TRIU_I, _TRIU_J = np.triu_indices(F + 1, k=1)
        _TRIU_I = jnp.asarray(_TRIU_I)
        _TRIU_J = jnp.asarray(_TRIU_J)
        combined = jnp.concatenate([sparse_x, dense_x[:, None, :]], axis=1)
        interact = jnp.einsum('bfd,bgd->bfg', combined, combined)
        return interact[:, _TRIU_I, _TRIU_J]
    e = jnp.stack([tbl_0[ids[:, 0]], tbl_1[ids[:, 1]], tbl_2[ids[:, 2]], tbl_3[ids[:, 3]], tbl_4[ids[:, 4]], tbl_5[ids[:, 5]], tbl_6[ids[:, 6]], tbl_7[ids[:, 7]], tbl_8[ids[:, 8]], tbl_9[ids[:, 9]], tbl_10[ids[:, 10]], tbl_11[ids[:, 11]], tbl_12[ids[:, 12]], tbl_13[ids[:, 13]], tbl_14[ids[:, 14]], tbl_15[ids[:, 15]], tbl_16[ids[:, 16]], tbl_17[ids[:, 17]], tbl_18[ids[:, 18]], tbl_19[ids[:, 19]], tbl_20[ids[:, 20]], tbl_21[ids[:, 21]], tbl_22[ids[:, 22]], tbl_23[ids[:, 23]], tbl_24[ids[:, 24]], tbl_25[ids[:, 25]]], axis=1)
    z = _L0_rec_ref(e, r_dense_x)
    z = z.reshape(z.shape[0], -1)
    h = jnp.concatenate([z, r_dense_x], axis=1)
    h = jnp.maximum(h @ W_top1 + b_top1, 0.0)
    h = jnp.maximum(h @ W_top2 + b_top2, 0.0)
    y = h @ W_top3
    return y

_drawn_inputs = setup_inputs


def setup_inputs(seed=0):
    import zlib

    import numpy as np

    out = dict(_drawn_inputs(seed))
    spreads = {'b_top1': (0.0, 0.1), 'b_top2': (0.0, 0.1)}
    factors = {}
    for name, (base, spread) in spreads.items():
        noise = np.random.default_rng([zlib.crc32(name.encode()), seed]).standard_normal(out[name].shape)
        drawn = base * np.exp(spread * noise) if base else spread * noise
        out[name] = jnp.asarray(drawn.astype(out[name].dtype))
    for name, factor in factors.items():
        out[name] = (out[name] * factor).astype(out[name].dtype)
    return out
```

```python
from contextlib import ExitStack

import concourse.bass as bass
from concourse import mybir

F32 = mybir.dt.float32
I32 = mybir.dt.int32
ALU = mybir.AluOpType
ACT = mybir.ActivationFunctionType

B, D, F = 2048, 128, 26
NF = F + 1
H1, H2 = 512, 256
P = 128
SLOT = 32
TILE = P
PAIR = 2 * TILE
STEPS = B // PAIR
S4 = P // SLOT
GROUPS = TILE // S4
QF = 4
QUADS = (NF + QF - 1) // QF
JB = 7
JS = S4 * JB
SETG = 8
SETS = GROUPS // SETG
BANKG = 4
N1, N2 = H1 // P, H2 // P
EVEN = {0: 0, 1: 4, 2: 7}


def quads_before(u, parity):
    return (QUADS * u + 1 - parity) // 2


def tower_kernel(nc, x, ids, tables, w1_pairs, w1_dense, w2, w3, b1, b2, out):
    ctx = ExitStack()
    with ctx:
        sb = lambda name, shape, dt=F32: ctx.enter_context(nc.sbuf_tensor(name, shape, dt))
        ps = lambda name, shape: ctx.enter_context(nc.psum_tensor(name, shape, F32))
        sem = lambda name: ctx.enter_context(nc.semaphore(name))

        ident = sb("ident", [P, P])
        w1z_sb = sb("w1z_sb", [P, JB, H1])
        w1x_sb = sb("w1x_sb", [P, H1])
        w2_sb = sb("w2_sb", [P, N1, H2])
        w3_sb = sb("w3_sb", [P, N2])
        b1_sb = sb("b1_sb", [P, N1])
        b2_sb = sb("b2_sb", [P, N2])
        idx = [sb(f"idx{u}", [P, F], I32) for u in range(2)]
        rows = [sb(f"rows{u}", [P, NF, D]) for u in range(2)]
        emb = [sb(f"emb{u}", [P, TILE, SLOT]) for u in range(2)]
        xT = sb("xT", [P, 2, S4, GROUPS])
        gram = [sb(f"gram{u}", [P, JS, GROUPS]) for u in range(2)]
        z = sb("z", [P, 2 * S4, JB, GROUPS])
        h1 = sb("h1", [P, N1, PAIR])
        h2 = sb("h2", [P, N2, PAIR])
        y_sb = sb("y_sb", [1, B])

        ps_t = [ps(f"ps_t{i}", [P, QF, TILE]) for i in range(2)]
        ps_g = [ps(f"ps_g{i}", [P, 2, 512]) for i in range(2)]
        ps_m = [ps(f"ps_m{i}", [P, 2, PAIR]) for i in range(2)]

        ident_made = sem("ident_made")
        weights_in = sem("weights_in")
        slots_zeroed = sem("slots_zeroed")
        room_seen = sem("room_seen")
        idx_in = [sem(f"idx_in{u}") for u in range(2)]
        x_in = [sem(f"x_in{u}") for u in range(2)]
        rows_in = [[sem(f"rows_in{u}_{k}") for k in range(QUADS)] for u in range(2)]
        quad_transposed = sem("quad_transposed")
        quad_moved = [sem("even_quad_moved"), sem("odd_quad_moved")]
        set_done = sem("set_done")
        set_moved = [sem("set_moved_dve"), sem("set_moved_act")]
        gram_spread = [sem(f"gram_spread{u}") for u in range(2)]
        w1_done = sem("w1_done")
        h1_made = sem("h1_made")
        w2_done = sem("w2_done")
        h2_made = sem("h2_made")
        w3_done = sem("w3_done")
        y_made = sem("y_made")
        y_out = sem("y_out")

        block = ctx.enter_context(nc.Block())
        x_t = x.rearrange("(t p) d -> t p d", p=TILE)
        ids_t = ids.rearrange("(t p) f -> t p f", p=TILE)
        out_row = out.rearrange("b o -> o b")
        quad_fields = [list(range(k * QF, min(NF, (k + 1) * QF))) for k in range(QUADS)]
        SPREADS = 16 * S4 * S4

        @block.gpsimd
        def _(pool):
            nc.gpsimd.memset(ident[:], 0.0).then_inc(ident_made, 1)
            pool.wait_ge(ident_made, 1)
            nc.gpsimd.affine_select(out=ident[:], in_=ident[:], compare_op=ALU.not_equal, fill=1.0, base=0,
                                    pattern=[[-1, P]], channel_multiplier=1).then_inc(ident_made, 1)

            def gather(t, first):
                for u in range(2):
                    pool.wait_ge(idx_in[u], 16 * t + 16)
                    for k in range(QUADS):
                        if not first:
                            pool.wait_ge(quad_transposed, 2 * QUADS * t - 2 * QUADS + QUADS * u + k + 1)
                            pool.sem_inc(room_seen, 1)
                        for f in quad_fields[k]:
                            if f < F:
                                pool.indirect_dma_start(
                                    out=rows[u][:, f, :], out_offset=None, in_=tables[f],
                                    in_offset=bass.IndirectOffsetOnAxis(ap=idx[u][:, f:f + 1], axis=0),
                                ).then_inc(rows_in[u][k], 16)

            gather(0, True)
            with pool.Fori(1, STEPS) as t:
                gather(t, False)

        @block.sync
        def _(sp):
            def load(t, u, first):
                if not first:
                    last = 16 * sum(f < F for f in quad_fields[-1])
                    sp.wait_ge(rows_in[u][QUADS - 1], last * t)
                sp.dma_start(idx[u][:], ids_t[2 * t + u]).then_inc(idx_in[u], 16)
                if not first:
                    sp.wait_ge(quad_transposed, 2 * QUADS * t - QUADS * (1 - u))
                sp.dma_start(rows[u][:, F, :], x_t[2 * t + u]).then_inc(x_in[u], 16)

            def spread(t, u, first):
                if not first and u == 0:
                    sp.wait_ge(w1_done, 2 * t)
                for e in range(2):
                    sp.wait_ge(set_moved[e], 2 * SETS * t + SETS * (u + 1))
                for s in range(S4):
                    for q in range(S4):
                        sp.dma_start(z[SLOT * q:SLOT * (q + 1), S4 * u + s, :, :],
                                     gram[u][SLOT * s:SLOT * (s + 1), JB * q:JB * (q + 1), :]
                                     ).then_inc(gram_spread[u], 16)

            def step(t, first, last):
                for u in range(2):
                    if not last:
                        load(t + 1, u, False)
                    spread(t, u, first)

            load(0, 0, True)
            load(0, 1, True)
            step(0, True, False)
            with sp.Fori(1, STEPS - 1) as t:
                step(t, False, False)
            step(STEPS - 1, False, True)
            sp.wait_ge(y_made, STEPS + 1)
            sp.dma_start(out_row, y_sb[:]).then_inc(y_out, 16)
            sp.wait_ge(y_out, 16)

        def move_quad(eng_wait, copy, t, u, k, first):
            m = QUADS * u + k
            eng_wait(quad_transposed, 2 * QUADS * t + m + 1)
            if k < 2:
                if not first:
                    eng_wait(set_done, 2 * SETS * t - 2 * SETS + SETS * (u + 1))
            n = len(quad_fields[k])
            dst = emb[u][:, :, k * QF:k * QF + n].rearrange("p b f -> p f b")
            if k == QUADS - 1:
                copy(xT[:, u], ps_t[m % 2][:, n - 1, :].rearrange("p (g s) -> p s g", s=S4))
            copy(dst, ps_t[m % 2][:, 0:n, :]).then_inc(quad_moved[m % 2], 1)

        def move_sets(eng_wait, copy, t, u, members, e, first):
            for c in range(SETS):
                eng_wait(set_done, 2 * SETS * t + SETS * u + c + 1)
                if c == 0 and not first:
                    eng_wait(gram_spread[u], SPREADS * t)
                for s in members:
                    for b in range(2):
                        src = ps_g[c % 2][SLOT * s:SLOT * (s + 1), b, 0:BANKG * S4 * NF].rearrange(
                            "p (g s j) -> p s j g", s=S4, j=NF)[:, s]
                        g0 = SETG * c + BANKG * b
                        last = copy(gram[u][SLOT * s:SLOT * (s + 1), 0:NF, g0:g0 + BANKG], src)
                last.then_inc(set_moved[e], 1)

        @block.vector
        def _(dve):
            nc.vector.memset(y_sb[:], 0.0).then_inc(y_made, 1)
            for u in range(2):
                nc.vector.memset(emb[u][:, :, NF:SLOT], 0.0)
                nc.vector.memset(gram[u][:, NF:JS, :], 0.0).then_inc(slots_zeroed, 1)

            def step(t, first):
                for u in range(2):
                    for k in range(QUADS):
                        if (QUADS * u + k) % 2 == 0:
                            move_quad(dve.wait_ge, nc.vector.tensor_copy, t, u, k, first)
                    move_sets(dve.wait_ge, nc.vector.tensor_copy, t, u, (0, 1), 0, first)
                    if u == 0 and not first:
                        finish(t - 1)

            def finish(t):
                dve.wait_ge(w3_done, t + 1)
                nc.vector.tensor_copy(y_sb[:, bass.ts(t, PAIR)].rearrange("o (u g s) -> o u s g", u=2, s=S4),
                                      ps_m[1][0:1, 0, :].rearrange("o (u s g) -> o u s g", u=2, s=S4)).then_inc(y_made, 1)

            step(0, True)
            with dve.Fori(1, STEPS) as t:
                step(t, False)
            finish(STEPS - 1)

        @block.scalar
        def _(act):
            for dst, src in ((b1_sb[:], b1), (b2_sb[:], b2), (w3_sb[:], w3), (w1z_sb[:], w1_pairs), (w1x_sb[:], w1_dense),
                             (w2_sb[:], w2)):
                act.dma_start(dst, src).then_inc(weights_in, 16)

            def layers(t):
                for n in range(N1):
                    act.wait_ge(w1_done, 2 * t + n // 2 + 1)
                    nc.scalar.activation(h1[:, n, :], ps_m[n // 2][:, n % 2, :], ACT.Relu,
                                         bias=b1_sb[:, n:n + 1]).then_inc(h1_made, 1)

            def layer2(t):
                act.wait_ge(w2_done, t + 1)
                for n in range(N2):
                    nc.scalar.activation(h2[:, n, :], ps_m[0][:, n, :], ACT.Relu,
                                         bias=b2_sb[:, n:n + 1]).then_inc(h2_made, 1)

            def step(t, first):
                for u in range(2):
                    for k in range(QUADS):
                        if u == 0 and k == QUADS - 1 and not first:
                            layers(t - 1)
                        if (QUADS * u + k) % 2 == 1:
                            move_quad(act.wait_ge, nc.scalar.copy, t, u, k, first)
                    move_sets(act.wait_ge, nc.scalar.copy, t, u, (2, 3), 1, first)
                    if u == 0 and not first:
                        layer2(t - 1)

            step(0, True)
            act.wait_ge(weights_in, 96)
            with act.Fori(1, STEPS) as t:
                step(t, False)
            layers(STEPS - 1)
            layer2(STEPS - 1)

        @block.tensor
        def _(pe):
            def transposes(t, u, k, first):
                m = QUADS * u + k
                if m >= 2 or not first:
                    pe.wait_ge(quad_moved[m % 2], QUADS * t + m // 2)
                pe.wait_ge(rows_in[u][k], 16 * sum(f < F for f in quad_fields[k]) * (t + 1))
                if k == QUADS - 1:
                    pe.wait_ge(x_in[u], 16 * t + 16)
                for i, f in enumerate(quad_fields[k]):
                    last = nc.tensor.transpose(ps_t[m % 2][:, i, :], rows[u][:, f, :], ident[:])
                last.then_inc(quad_transposed, 1)

            def products(t, u, first):
                for e in range(2):
                    pe.wait_ge(quad_moved[e], QUADS * t + quads_before(u + 1, e))
                for c in range(SETS):
                    if c >= 2 or u == 1 or not first:
                        for e in range(2):
                            pe.wait_ge(set_moved[e], 2 * SETS * t + SETS * u + c - 1)
                    for i in range(SETG):
                        g = SETG * c + i
                        o = (i % BANKG) * S4 * NF
                        last = nc.tensor.matmul(ps_g[c % 2][:, i // BANKG, o:o + S4 * NF],
                                                emb[u][:, S4 * g:S4 * (g + 1), :].rearrange("p s f -> p (s f)"),
                                                emb[u][:, S4 * g:S4 * (g + 1), 0:NF], start=True, stop=True)
                    last.then_inc(set_done, 1)

            def layer1(t):
                for u in range(2):
                    pe.wait_ge(gram_spread[u], SPREADS * t + SPREADS)
                for n in range(N1):
                    if n == N1 // 2:
                        pe.wait_ge(y_made, t + 1)
                    to, cols = ps_m[n // 2][:, n % 2, :], slice(P * n, P * (n + 1))
                    for jj in range(JB):
                        nc.tensor.matmul(to, w1z_sb[:, jj, cols], z[:, :, jj, :], start=jj == 0, stop=False)
                    last = nc.tensor.matmul(to, w1x_sb[:, cols], xT[:].rearrange("p u s g -> p (u s g)"), start=False, stop=True)
                    if n % 2:
                        last.then_inc(w1_done, 1)

            def layer2(t):
                for n in range(N2):
                    for c in range(N1):
                        if n == 0:
                            pe.wait_ge(h1_made, N1 * t + N1)
                        last = nc.tensor.matmul(ps_m[0][:, n, :], w2_sb[:, c, P * n:P * (n + 1)], h1[:, c, :],
                                                start=c == 0, stop=c == N1 - 1)
                last.then_inc(w2_done, 1)

            def layer3(t):
                pe.wait_ge(h2_made, N2 * t + N2)
                for n in range(N2):
                    last = nc.tensor.matmul(ps_m[1][0:1, 0, :], w3_sb[:, n:n + 1], h2[:, n, :], start=n == 0, stop=n == N2 - 1)
                last.then_inc(w3_done, 1)

            def step(t, first):
                for u in range(2):
                    for k in range(QUADS):
                        if u == 0 and k == QUADS - 1 and not first:
                            layer1(t - 1)
                        transposes(t, u, k, first)
                    products(t, u, first)
                    if u == 0 and not first:
                        layer2(t - 1)
                        layer3(t - 1)

            pe.wait_ge(ident_made, 2)
            pe.wait_ge(slots_zeroed, 2)
            pe.wait_ge(weights_in, 96)
            step(0, True)
            with pe.Fori(1, STEPS) as t:
                step(t, False)
            layer1(STEPS - 1)
            layer2(STEPS - 1)
            layer3(STEPS - 1)


def kernel(**inputs):
    import numpy as np
    import concourse.bacc as bacc
    from concourse.bass_utils import run_bass_kernel_spmd

    arrays = {name: np.ascontiguousarray(a) for name, a in inputs.items()}
    w1 = arrays.pop("W_top1")
    pairs = NF * (NF - 1) // 2
    i, j = np.triu_indices(NF, k=1)
    laid = np.zeros((S4, SLOT, JB, H1), w1.dtype)
    laid[j // JB, i, j % JB] = w1[:pairs]
    arrays["w1_pairs"] = laid.reshape(P, JB, H1)
    arrays["w1_dense"] = np.ascontiguousarray(w1[pairs:])
    arrays["w2"] = np.ascontiguousarray(arrays.pop("W_top2").reshape(N1, P, H2).transpose(1, 0, 2))
    arrays["w3"] = np.ascontiguousarray(arrays.pop("W_top3").reshape(N2, P).T)
    arrays["b1"] = np.ascontiguousarray(arrays.pop("b_top1").reshape(N1, P).T)
    arrays["b2"] = np.ascontiguousarray(arrays.pop("b_top2").reshape(N2, P).T)

    nc = bacc.Bacc("TRN2", target_bir_lowering=False, num_devices=1)
    ap = {name: nc.dram_tensor(name, a.shape, mybir.dt.from_np(a.dtype), kind="ExternalInput").ap()
          for name, a in arrays.items()}
    out = nc.dram_tensor("y", (B, 1), F32, kind="ExternalOutput").ap()
    tower_kernel(nc, ap["r_dense_x"], ap["ids"], [ap[f"tbl_{f}"] for f in range(F)], ap["w1_pairs"], ap["w1_dense"],
                 ap["w2"], ap["w3"], ap["b1"], ap["b2"], out)
    return run_bass_kernel_spmd(nc, [arrays], core_ids=[0]).results[0]["y"]
```

```python
from contextlib import ExitStack

import concourse.bass as bass
from concourse import mybir

F32 = mybir.dt.float32
F32R = mybir.dt.float32r
I32 = mybir.dt.int32
ALU = mybir.AluOpType
ACT = mybir.ActivationFunctionType

B, D, F = 2048, 128, 26
NF = F + 1
H1, H2 = 512, 256
P = 128
SLOT = 32
TILE = P
PAIR = 2 * TILE
STEPS = B // PAIR
S4 = P // SLOT
GROUPS = TILE // S4
JB = 7
JS = S4 * JB
GW = 256
SETG = 4
SETS = GROUPS // SETG
N1, N2 = H1 // P, H2 // P

OH_FIELDS = (6, 7, 9, 10, 11, 12)
OH_ROWS = 1000
KT = 8
OH_P = OH_ROWS // KT
KH = KT // 2
NOH = len(OH_FIELDS)
ITEMS = [list(range(i, min(NOH, i + 2))) for i in range(0, NOH, 2)]
NI = len(ITEMS)
FILLS = [(i, k, 4 // len(tb)) for i, tb in enumerate(ITEMS) for k in range(0, KT, 4 // len(tb))]
NFILL = len(FILLS)
BUFS = 3
EARLY = NI - 1
EARLY_T = ITEMS[EARLY - 1][-1] + 1
AHEAD = 8
GATHERED = tuple(f for f in range(F) if f not in OH_FIELDS)
NG = len(GATHERED)
XS = NG
OS = NG + 1
SLOT_OF = GATHERED + (F,) + OH_FIELDS
QF = 4
QUAD_SLOTS = [range(XS, XS + 1)] + [range(v, v + QF) for v in range(0, NG, QF)]
QUADS = len(QUAD_SLOTS)
assert NG % QF == 0 and QUADS % 2 == 0 and NFILL % BUFS == 0 and NFILL == 12 and AHEAD == SETS

LATE = [("quad", 0), ("quad", 1), ("fill", 8), ("quad", 2), ("fill", 9), ("fill", 10), ("quad", 3), ("fill", 11),
        ("quad", 4), ("quad", 5)]
ALL_FILLS = [("fill", h) for h in range(AHEAD)]
L1_PARTS = SETS - 1


def tower_kernel(nc, x, ids, ids_oh, gathered, oh_tables, w1_pairs, w1_dense, w2, w3, b1, b2, out):
    ctx = ExitStack()
    with ctx:
        sb = lambda name, shape, dt=F32: ctx.enter_context(nc.sbuf_tensor(name, shape, dt))
        ps = lambda name, shape: ctx.enter_context(nc.psum_tensor(name, shape, F32))
        sem = lambda name: ctx.enter_context(nc.semaphore(name))

        ident = sb("ident", [P, P])
        first_row_i = sb("first_row_i", [P, 1], I32)
        first_row = sb("first_row", [P, 1])
        tab = sb("tab", [P, NOH, 2, KT, D], F32R)
        w1_sb = sb("w1_sb", [P, 2, JB + 1, H1], F32R)
        w2_sb = sb("w2_sb", [P, 2, N1, H2], F32R)
        w3_sb = sb("w3_sb", [P, N2])
        b1_sb = sb("b1_sb", [P, N1])
        b2_sb = sb("b2_sb", [P, N2])
        idx = [sb(f"idx{u}", [P, F], I32) for u in range(2)]
        rows = [sb(f"rows{u}", [P, NG + 1, D]) for u in range(2)]
        ids_b = sb("ids_b", [P, NOH, PAIR])
        onehot = [sb(f"onehot{r}", [P, 4 * PAIR], F32R) for r in range(BUFS)]
        emb = sb("emb", [P, GROUPS, 2, S4, SLOT], F32R)
        held = [sb("held0", [P, EARLY_T, TILE]),
                sb("held1", [P, NOH, TILE])]
        x_held = sb("x_held", [P, 2, S4, GROUPS], F32R)
        xz = sb("xz", [P, 2, 2, S4, GROUPS], F32R)
        gram = [sb(f"gram{u}", [P, JS, GROUPS]) for u in range(2)]
        zh = sb("zh", [P, 2, S4, JB, GROUPS], F32R)
        zl = sb("zl", [P, 2, S4, JB, GROUPS], F32R)
        h1 = sb("h1", [P, N1, PAIR])
        h1h = sb("h1h", [P, N1, PAIR], F32R)
        h1l = sb("h1l", [P, N1, PAIR], F32R)
        stage = sb("stage", [P, 512])
        h2 = h1[:, 0:N2, :]
        y_sb = sb("y_sb", [P, 2 * STEPS])
        y_rows = sb("y_rows", [2 * STEPS, TILE])
        turn = [nc.dram_tensor(f"turn{u}", (S4, SLOT, S4, JB * GROUPS), F32).ap() for u in range(2)]

        ps_t = [ps(f"ps_t{i}", [P, QF, TILE]) for i in range(2)]
        ps_g = [ps(f"ps_g{i}", [P, SETG, GW]) for i in range(2)]
        ps_m = [ps(f"ps_m{i}", [P, 2, PAIR]) for i in range(2)]

        consts_made = sem("consts_made")
        small_in = sem("small_in")
        chunk_in = [sem(f"chunk_in{r}") for r in range(10)]
        chunk_h = sem("chunk_h")
        chunk_l = sem("chunk_l")
        pads_zeroed = sem("pads_zeroed")
        room_seen = sem("room_seen")
        idx_in = [sem(f"idx_in{u}") for u in range(2)]
        ids_in = sem("ids_in")
        ids_less = sem("ids_less")
        x_in = [sem(f"x_in{u}") for u in range(2)]
        rows_in = [[sem(f"rows_in{u}_{k}") for k in range(QUADS)] for u in range(2)]
        onehot_made = sem("onehot_made")
        onehot_used = sem("onehot_used")
        item_out = sem("item_out")
        item_l = sem("item_l")
        held_h = sem("held_h")
        held_l = sem("held_l")
        quad_transposed = sem("quad_transposed")
        quad_h = sem("quad_h")
        quad_l = sem("quad_l")
        x_kept = sem("x_kept")
        set_done = sem("set_done")
        set_h = sem("set_h")
        set_moved = sem("set_moved")
        gram_out = [sem(f"gram_out{u}") for u in range(2)]
        z_in = [sem(f"z_in{u}") for u in range(2)]
        z_h = sem("z_h")
        z_l = sem("z_l")
        w1_done = sem("w1_done")
        h1_h = sem("h1_h")
        h1_l = sem("h1_l")
        w2_done = sem("w2_done")
        h2_made = sem("h2_made")
        w3_done = sem("w3_done")
        y_made = sem("y_made")
        y_turned = sem("y_turned")
        y_out = sem("y_out")

        block = ctx.enter_context(nc.Block())
        f32 = lambda ap: ap.bitcast(F32)
        x_t = x.rearrange("(t p) d -> t p d", p=TILE)
        ids_t = ids.rearrange("(t p) f -> t p f", p=TILE)
        ROWS_IN = 16 * QF
        fills_to = [max(h for h, f in enumerate(FILLS) if f[0] == i) + 1 for i in range(NI)]
        ends_item = {n - 1: i for i, n in enumerate(fills_to)}

        chunks = []
        for n in range(NOH):
            rows_of = oh_tables[n].rearrange("(p k) d -> p k d", k=KT)
            for a in range(2):
                ks = slice(KH * a, KH * (a + 1))
                chunks.append((rows_of[:, ks, :], OH_P, tab[0:OH_P, n, 0, ks, :], tab[0:OH_P, n, 1, ks, :]))
        TAB_CHUNKS = len(chunks)
        for jj in range(JB + 1):
            src = w1_pairs[:, jj, :] if jj < JB else w1_dense
            chunks.append((src, P, w1_sb[:, 0, jj, :], w1_sb[:, 1, jj, :]))
        for a in range(2):
            cs = slice(a * N1 // 2, (a + 1) * N1 // 2)
            chunks.append((w2[:, cs, :], P, w2_sb[:, 0, cs, :], w2_sb[:, 1, cs, :]))
        STAGES = [h1[:, 2 * x:2 * x + 2, :].rearrange("p a b -> p (a b)") for x in range(2)] + [stage[:]]
        NW = len(STAGES)
        STAGES += [g[:].rearrange("p j g -> p (j g)")[:, 0:512] for g in gram]
        STAGES += [rows[1][:, 4 * x:4 * x + 4, :].rearrange("p v d -> p (v d)") for x in range(NG // 4)]
        NS = len(STAGES)

        def stage_of(c):
            return c % NS if c < TAB_CHUNKS else (c - TAB_CHUNKS) % NW

        def chunks_in(c):
            before = [b for b in range(c) if stage_of(b) == stage_of(c)]
            return len(before) + 1, before[-1] + 1 if before else 0

        def staged(c):
            _, parts, hi, _ = chunks[c]
            at = STAGES[stage_of(c)][0:parts, :]
            return at if len(hi.shape) == 2 else at.rearrange("p (a b) -> p a b", a=hi.shape[1])

        def tables_beside(h):
            return range(2 * len(ITEMS[0]) * (h + 2) // 2, min(TAB_CHUNKS, 2 * len(ITEMS[0]) * (h + 3) // 2))

        def weights_beside(c):
            n = len(chunks) - TAB_CHUNKS
            return range(TAB_CHUNKS + n * c // SETS, TAB_CHUNKS + n * (c + 1) // SETS)

        def by_vector(part, a, b):
            return emb[:, :, part, :, a:b].rearrange("p g s f -> p f g s")

        def grouped(ap):
            return ap.rearrange("p f (g s) -> p f g s", s=S4)

        def columns(h):
            _, _, kb = FILLS[h]
            return onehot[h % BUFS][0:OH_P, :].rearrange("p (k n b) -> p k n b", k=kb, b=PAIR)

        @block.gpsimd
        def _(pool):
            nc.gpsimd.memset(ident[:], 0.0).then_inc(consts_made, 1)
            pool.wait_ge(consts_made, 1)
            nc.gpsimd.affine_select(out=ident[:], in_=ident[:], compare_op=ALU.not_equal, fill=1.0, base=0,
                                    pattern=[[-1, P]], channel_multiplier=1).then_inc(consts_made, 1)
            nc.gpsimd.iota(first_row_i[:], pattern=[[1, 1]], base=0, channel_multiplier=-KT).then_inc(consts_made, 1)

            def gather(t, first):
                for u in range(2):
                    pool.wait_ge(idx_in[u], 16 * t + 16)
                    if first and u == 1:
                        pool.wait_ge(chunk_l, TAB_CHUNKS)
                        pool.sem_inc(room_seen, 1)
                    for k in range(1, QUADS):
                        if not first:
                            pool.wait_ge(quad_transposed, 2 * QUADS * t - 2 * QUADS + QUADS * u + k + 1)
                            pool.sem_inc(room_seen, 1)
                        for v in QUAD_SLOTS[k]:
                            f = GATHERED[v]
                            pool.indirect_dma_start(
                                out=rows[u][:, v, :], out_offset=None, in_=gathered[v],
                                in_offset=bass.IndirectOffsetOnAxis(ap=idx[u][:, f:f + 1], axis=0),
                            ).then_inc(rows_in[u][k], 16)

            gather(0, True)
            with pool.Fori(1, STEPS) as t:
                gather(t, False)

        @block.sync
        def _(sp):
            def load_idx(t, u, first):
                if not first:
                    sp.wait_ge(rows_in[u][QUADS - 1], ROWS_IN * t)
                sp.dma_start(idx[u][:], ids_t[2 * t + u]).then_inc(idx_in[u], 16)

            def load_x(t, u, first):
                if not first:
                    sp.wait_ge(quad_transposed, 2 * QUADS * t - 2 * QUADS + QUADS * u + 1)
                sp.dma_start(rows[u][:, XS, :], x_t[2 * t + u]).then_inc(x_in[u], 16)

            def load_ids(t, first):
                if not first:
                    sp.wait_ge(onehot_made, NFILL * t)
                sp.dma_start(ids_b[:].bitcast(I32), ids_oh[:, bass.ts(t, PAIR)].partition_broadcast(P)
                             ).then_inc(ids_in, 16)

            def spread(t, u):
                sp.wait_ge(set_moved, 2 * SETS * t + SETS * (u + 1))
                for s in range(S4):
                    sp.dma_start(turn[u][:, :, s, :].rearrange("q i c -> i q c"),
                                 gram[u][SLOT * s:SLOT * (s + 1), :, :].rearrange("i (q j) g -> i q (j g)", q=S4)
                                 ).then_inc(gram_out[u], 16)

            def gather_z(t, u, first):
                if not first and u == 0:
                    sp.wait_ge(w1_done, 2 * t)
                sp.wait_ge(gram_out[u], 16 * S4 * t + 16 * S4)
                sp.dma_start(f32(zl[:, u]).rearrange("p s j g -> p (s j g)"),
                             turn[u].rearrange("q i s c -> (q i) (s c)")).then_inc(z_in[u], 16)

            def step(t, first, last):
                if not last:
                    load_idx(t + 1, 0, False)
                if not first:
                    spread(t - 1, 1)
                    gather_z(t - 1, 1, False)
                if not last:
                    load_x(t + 1, 0, False)
                    load_ids(t + 1, False)
                if first:
                    for c in range(TAB_CHUNKS, len(chunks)):
                        load_chunk(c)
                if not last:
                    load_idx(t + 1, 1, False)
                spread(t, 0)
                gather_z(t, 0, first)
                if not last:
                    load_x(t + 1, 1, False)

            def load_chunk(c):
                n, before = chunks_in(c)
                if before:
                    sp.wait_ge(chunk_l, before)
                sp.dma_start(staged(c), chunks[c][0]).then_inc(chunk_in[stage_of(c)], 16)

            load_idx(0, 0, True)
            load_chunk(0)
            load_ids(0, True)
            for c in range(1, TAB_CHUNKS):
                load_chunk(c)
                if c == 4:
                    load_idx(0, 1, True)
                    load_x(0, 0, True)
            load_x(0, 1, True)
            step(0, True, False)
            with sp.Fori(1, STEPS - 1) as t:
                step(t, False, False)
            step(STEPS - 1, False, True)
            spread(STEPS - 1, 1)
            gather_z(STEPS - 1, 1, False)
            sp.wait_ge(y_made, STEPS + 1)
            sp.dma_start(out.rearrange("(t p) o -> t (p o)", p=TILE), y_rows[:]).then_inc(y_out, 16)
            sp.wait_ge(y_out, 16)

        @block.scalar
        def _(act):
            def chunk(c):
                act.wait_ge(chunk_in[stage_of(c)], 16 * chunks_in(c)[0])
                nc.scalar.copy(chunks[c][2], staged(c)).then_inc(chunk_h, 1)

            def less(t):
                act.wait_ge(ids_in, 16 * t + 16)
                nc.scalar.activation(ids_b[:], ids_b[:].bitcast(I32), ACT.Identity,
                                     bias=first_row[:, 0:1]).then_inc(ids_less, 1)

            def item(t, i):
                act.wait_ge(onehot_used, NFILL * t + fills_to[i])
                a, n = ITEMS[i][0], len(ITEMS[i])
                nc.scalar.copy(held[1][:, a:a + n, :], ps_m[i % 2][:, 0:n, TILE:PAIR])
                src = ps_m[i % 2][:, 0:n, 0:TILE]
                if i < EARLY:
                    nc.scalar.copy(held[0][:, a:a + n, :], src).then_inc(item_out, 1)
                else:
                    nc.scalar.copy(by_vector(0, OS + a, OS + a + n), grouped(src)).then_inc(item_out, 1)

            def unhold(t, u):
                act.wait_ge(item_out, NI * t + (NI if u else EARLY))
                n = held[u].shape[1]
                nc.scalar.copy(by_vector(0, OS, OS + n), grouped(held[u][:])).then_inc(held_h, 1)

            def quad(t, u, k):
                m = QUADS * u + k
                act.wait_ge(quad_transposed, 2 * QUADS * t + m + 1)
                a, n = QUAD_SLOTS[k][0], len(QUAD_SLOTS[k])
                nc.scalar.copy(by_vector(0, a, a + n), grouped(ps_t[m % 2][:, 0:n])).then_inc(quad_h, 1)

            def move_set(t, u, c, first):
                act.wait_ge(set_done, 2 * SETS * t + SETS * u + c + 1)
                if c == 0 and not first:
                    act.wait_ge(gram_out[u], 16 * S4 * t)
                for s in range(S4):
                    ss = slice(SLOT * s, SLOT * (s + 1))
                    last = nc.scalar.activation(
                        gram[u][ss, 0:NF, SETG * c:SETG * (c + 1)].rearrange("p j g -> p g j"),
                        ps_g[c % 2][ss, :, JS * s:JS * s + NF], ACT.Copy, scale=0.5)
                last.then_inc(set_h, 1)

            def split_z(t, u):
                act.wait_ge(z_in[u], 16 * t + 16)
                nc.scalar.copy(zh[:, u], f32(zl[:, u])).then_inc(z_h, 1)

            def layer1(t, bank):
                act.wait_ge(w1_done, 2 * t + bank + 1)
                for i in range(2):
                    n = 2 * bank + i
                    for to in (h1, h1h):
                        last = nc.scalar.activation(to[:, n, :], ps_m[bank][:, i, :], ACT.Relu, bias=b1_sb[:, n:n + 1])
                    last.then_inc(h1_h, 1)

            def layer2(t):
                act.wait_ge(w2_done, t + 1)
                for n in range(N2):
                    last = nc.scalar.activation(h2[:, n, :], ps_m[1][:, n, :], ACT.Relu, bias=b2_sb[:, n:n + 1])
                last.then_inc(h2_made, 1)

            def step(t, first, last):
                if not first:
                    act.wait_ge(set_done, 2 * SETS * t)
                    act.wait_ge(x_kept, 2 * t)
                    act.wait_ge(held_l, 2 * t)
                for what, k in (ALL_FILLS if first else []) + LATE:
                    if what == "quad":
                        quad(t, 0, k)
                        if k == 1 and not first:
                            unhold(t, 0)
                    elif k in ends_item:
                        item(t, ends_item[k])
                        if first and ends_item[k] == EARLY - 1:
                            unhold(t, 0)
                if first:
                    act.wait_ge(chunk_l, TAB_CHUNKS)
                if not first:
                    split_z(t - 1, 1)
                for c in range(SETS):
                    move_set(t, 0, c, first)
                    if first:
                        for w in weights_beside(c):
                            chunk(w)
                    if c == 2 and not last:
                        less(t + 1)
                    if c == 4 and not first:
                        layer1(t - 1, 0)
                act.wait_ge(x_kept, 2 * t + 1)
                for k in range(QUADS):
                    quad(t, 1, k)
                    if k == 1:
                        unhold(t, 1)
                    if k == 3 and not first:
                        layer1(t - 1, 1)
                for c in range(SETS):
                    move_set(t, 1, c, first)
                    if c == 2 and not first:
                        layer2(t - 1)
                    if c == 3:
                        split_z(t, 0)
                    if not last and c == fills_to[0] + 1:
                        act.wait_ge(held_l, 2 * t + 2)
                        item(t + 1, 0)
                if not last:
                    item(t + 1, EARLY - 1)

            for dst, src in ((b1_sb, b1), (b2_sb, b2), (w3_sb, w3)):
                act.dma_start(dst[:], src).then_inc(small_in, 16)
            act.wait_ge(consts_made, 4)
            chunk(0)
            less(0)
            for c in range(1, TAB_CHUNKS):
                chunk(c)
            act.wait_ge(small_in, 48)
            step(0, True, False)
            with act.Fori(1, STEPS - 1) as t:
                step(t, False, False)
            step(STEPS - 1, False, True)
            split_z(STEPS - 1, 1)
            layer1(STEPS - 1, 0)
            layer1(STEPS - 1, 1)
            layer2(STEPS - 1)

        @block.vector
        def _(dve):
            def chunk(c):
                dve.wait_ge(chunk_h, c + 1)
                _, _, hi, lo = chunks[c]
                nc.vector.tensor_tensor(lo, staged(c), f32(hi), ALU.subtract).then_inc(chunk_l, 1)

            def fill(t, h, first):
                i, k0, kb = FILLS[h]
                if h == 0:
                    dve.wait_ge(ids_less, t + 1)
                if h >= BUFS or not first:
                    dve.wait_ge(onehot_used, NFILL * t + h - BUFS + 1)
                for k in range(kb):
                    a, n = ITEMS[i][0], len(ITEMS[i])
                    last = nc.vector.tensor_scalar(columns(h)[:, k], ids_b[0:OH_P, a:a + n, :], float(k0 + k), None,
                                                   ALU.is_equal)
                last.then_inc(onehot_made, 1)

            def item(t, i):
                dve.wait_ge(item_out, NI * t + i + 1)
                a, n = OS + ITEMS[i][0], OS + ITEMS[i][-1] + 1
                nc.vector.tensor_tensor(by_vector(1, a, n), grouped(ps_m[i % 2][:, 0:n - a, 0:TILE]),
                                        f32(by_vector(0, a, n)), ALU.subtract).then_inc(item_l, 1)

            def unhold(t, u):
                dve.wait_ge(held_h, 2 * t + u + 1)
                n = held[u].shape[1]
                nc.vector.tensor_tensor(by_vector(1, OS, OS + n), grouped(held[u][:]), f32(by_vector(0, OS, OS + n)),
                                        ALU.subtract).then_inc(held_l, 1)

            def quad(t, u, k):
                m = QUADS * u + k
                a, n = QUAD_SLOTS[k][0], QUAD_SLOTS[k][-1] + 1
                dve.wait_ge(quad_h, 2 * QUADS * t + m + 1)
                nc.vector.tensor_tensor(by_vector(1, a, n), grouped(ps_t[m % 2][:, 0:n - a]), f32(by_vector(0, a, n)),
                                        ALU.subtract).then_inc(quad_l, 1)

            def keep_x(t, u):
                dve.wait_ge(quad_l, 2 * QUADS * t + QUADS * u + 1)
                to = xz[:, :, 1] if u else x_held[:]
                nc.vector.tensor_copy(to.rearrange("p h s g -> p g h s"), f32(emb[:, :, :, :, XS])).then_inc(x_kept, 1)

            def unhold_x(t, first):
                if not first:
                    dve.wait_ge(w1_done, 2 * t)
                dve.wait_ge(x_kept, 2 * t + 1)
                nc.vector.tensor_copy(xz[:, :, 0], f32(x_held[:]))

            def move_set(t, u, c):
                dve.wait_ge(set_h, 2 * SETS * t + SETS * u + c + 1)
                for s in range(S4):
                    ss = slice(SLOT * s, SLOT * (s + 1))
                    to = gram[u][ss, 0:NF, SETG * c:SETG * (c + 1)].rearrange("p j g -> p g j")
                    last = nc.vector.tensor_tensor(to, ps_g[c % 2][ss, :, JS * (S4 + s):JS * (S4 + s) + NF], to, ALU.add)
                last.then_inc(set_moved, 1)

            def split_z(t, u):
                dve.wait_ge(z_h, 2 * t + u + 1)
                nc.vector.tensor_tensor(zl[:, u], f32(zl[:, u]), f32(zh[:, u]), ALU.subtract).then_inc(z_l, 1)

            def layer1(t, bank):
                for n in range(2 * bank, 2 * bank + 2):
                    dve.wait_ge(h1_h, N1 * t + n + 1)
                    nc.vector.tensor_tensor(h1l[:, n, :], h1[:, n, :], f32(h1h[:, n, :]), ALU.subtract).then_inc(h1_l, 1)

            def keep_y(t):
                dve.wait_ge(w3_done, t + 1)
                nc.vector.tensor_copy(y_sb[:, bass.ts(t, 2)], ps_m[1][:, 0, 0:2]).then_inc(y_made, 1)

            def step(t, first, last):
                if first:
                    for h in range(BUFS):
                        fill(t, h, True)
                else:
                    fill(t, NFILL - 2, False)
                for what, k in (ALL_FILLS if first else []) + LATE:
                    if what == "quad":
                        quad(t, 0, k)
                        if k == 1 and not first:
                            unhold(t, 0)
                        continue
                    if k + BUFS < NFILL:
                        fill(t, k + BUFS, first)
                    if k in ends_item and k >= AHEAD:
                        item(t, ends_item[k])
                    if first and k == fills_to[EARLY - 1] - 1:
                        unhold(t, 0)
                    if first:
                        for c in tables_beside(k):
                            chunk(c)
                keep_x(t, 0)
                if first:
                    for u in range(2):
                        nc.vector.memset(gram[u][:, NF:JS, :], 0.0)
                if not first:
                    split_z(t - 1, 1)
                for c in range(SETS):
                    move_set(t, 0, c)
                    if first:
                        for w in weights_beside(c):
                            chunk(w)
                    if c == 4 and not first:
                        layer1(t - 1, 0)
                    if c in (3, 4, 5) and not last:
                        fill(t + 1, c - 3, False)
                for k in range(QUADS):
                    quad(t, 1, k)
                    if k == 1:
                        unhold(t, 1)
                    if k == 3 and not first:
                        layer1(t - 1, 1)
                unhold_x(t, first)
                keep_x(t, 1)
                for c in range(SETS):
                    move_set(t, 1, c)
                    if not last and c > 0:
                        fill(t + 1, c + BUFS - 1, False)
                    if c == 3 and not first:
                        keep_y(t - 1)
                    if c == 3:
                        split_z(t, 0)

            nc.vector.memset(f32(emb[:, :, :, :, NF:SLOT].rearrange("p g h s f -> p (g h s) f")), 0.0
                             ).then_inc(pads_zeroed, 1)
            dve.wait_ge(consts_made, 3)
            nc.vector.tensor_copy(first_row[:], first_row_i[:]).then_inc(consts_made, 1)
            for c in range(2 * len(ITEMS[0])):
                chunk(c)
            step(0, True, False)
            with dve.Fori(1, STEPS - 1) as t:
                step(t, False, False)
            step(STEPS - 1, False, True)
            split_z(STEPS - 1, 1)
            layer1(STEPS - 1, 0)
            layer1(STEPS - 1, 1)
            keep_y(STEPS - 1)
            dve.wait_ge(y_turned, 1)
            nc.vector.tensor_copy(y_rows[:].rearrange("t (g s) -> t s g", s=S4),
                                  ps_t[0][0:2 * STEPS, 0, :].rearrange("t (s g) -> t s g", s=S4)).then_inc(y_made, 1)

        @block.tensor
        def _(pe):
            def fill(t, h, first):
                i, k0, kb = FILLS[h]
                if i == 1 and h == fills_to[0] and not first:
                    pe.wait_ge(y_made, t - 1)
                if i >= 2 and h == fills_to[i - 1]:
                    pe.wait_ge(item_out, NI * t + i - 1)
                pe.wait_ge(onehot_made, NFILL * t + h + 1)
                for k in range(kb):
                    for n, tb in enumerate(ITEMS[i]):
                        for part in range(2):
                            last = nc.tensor.matmul(ps_m[i % 2][:, n, :], tab[0:OH_P, tb, part, k0 + k, :],
                                                    columns(h)[:, k, n, :], start=(k0, k, n, part) == (0, 0, 0, 0),
                                                    stop=(k0 + k, n, part) == (KT - 1, len(ITEMS[i]) - 1, 1),
                                                    skip_group_check=True)
                last.then_inc(onehot_used, 1)

            def quad(t, u, k, first):
                m = QUADS * u + k
                if m >= 2 or not first:
                    pe.wait_ge(quad_l, 2 * QUADS * t + m - 1)
                if k == 0:
                    pe.wait_ge(x_in[u], 16 * t + 16)
                else:
                    pe.wait_ge(rows_in[u][k], ROWS_IN * t + ROWS_IN)
                for i, v in enumerate(QUAD_SLOTS[k]):
                    last = nc.tensor.transpose(ps_t[m % 2][:, i, :], rows[u][:, v, :], ident[:])
                last.then_inc(quad_transposed, 1)

            def products(t, u, c, first):
                if c == 0:
                    pe.wait_ge(quad_l, 2 * QUADS * t + QUADS * (u + 1))
                    pe.wait_ge(held_l, 2 * t + u + 1)
                    if u == 0:
                        pe.wait_ge(item_l, (NI - EARLY) * t + NI - EARLY)
                if c >= 2 or u == 1 or not first:
                    pe.wait_ge(set_moved, 2 * SETS * t + SETS * u + c - 1)
                for i in range(SETG):
                    g = SETG * c + i
                    last = nc.tensor.matmul(ps_g[c % 2][:, i, 0:2 * S4 * JS],
                                            emb[:, g, 0].rearrange("p s f -> p (s f)"),
                                            emb[:, g, :, :, 0:JS].rearrange("p h s f -> p (h s) f"),
                                            start=True, stop=True)
                last.then_inc(set_done, 1)

            def terms(w, blocks, n):
                cols = slice(P * n, P * (n + 1))
                return [(w[:, wp, b, cols], v[vp]) for wp, vp in ((0, 0), (0, 1), (1, 0)) for b, v in enumerate(blocks)]

            z_blocks = [[v[:, :, :, jj, :].rearrange("p u s g -> p (u s) g") for v in (zh, zl)] for jj in range(JB)]
            z_blocks.append([xz[:, h].rearrange("p u s g -> p (u s g)") for h in range(2)])
            L1 = [(n, i, *lr) for n in range(N1) for i, lr in enumerate(terms(w1_sb, z_blocks, n))]
            per_block = len(L1) // N1

            def layer1(t, part, parts):
                if part == 0:
                    pe.wait_ge(z_l, 2 * t + 2)
                    pe.wait_ge(x_kept, 2 * t + 2)
                for n, i, lhs, rhs in L1[part * len(L1) // parts:(part + 1) * len(L1) // parts]:
                    last = nc.tensor.matmul(ps_m[n // 2][:, n % 2, :], lhs, rhs, start=i == 0, stop=i == per_block - 1)
                    if n % 2 and i == per_block - 1:
                        last.then_inc(w1_done, 1)

            def layer2(t, n):
                if n == 0:
                    pe.wait_ge(h1_l, N1 * t + N1)
                tt = terms(w2_sb, [(h1h[:, c, :], h1l[:, c, :]) for c in range(N1)], n)
                for i, (lhs, rhs) in enumerate(tt):
                    last = nc.tensor.matmul(ps_m[1][:, n, :], lhs, rhs, start=i == 0, stop=i == len(tt) - 1)
                if n == N2 - 1:
                    last.then_inc(w2_done, 1)

            def layer3(t):
                pe.wait_ge(h2_made, t + 1)
                for u in range(2):
                    for n in range(N2):
                        last = nc.tensor.matmul(ps_m[1][:, 0, u:u + 1], h2[:, n, TILE * u:TILE * (u + 1)],
                                                w3_sb[:, n:n + 1], start=n == 0, stop=n == N2 - 1)
                last.then_inc(w3_done, 1)

            def step(t, first, last):
                for what, k in (ALL_FILLS if first else []) + LATE:
                    if what == "quad":
                        quad(t, 0, k, first)
                    elif what == "fill":
                        if first and FILLS[k][1] == 0:
                            pe.wait_ge(chunk_l, 2 * ITEMS[FILLS[k][0]][-1] + 2)
                        fill(t, k, True)
                for c in range(SETS):
                    if 2 <= c and not first:
                        layer1(t - 1, c - 2, L1_PARTS)
                    products(t, 0, c, first)
                for k in range(QUADS):
                    quad(t, 1, k, first)
                    if k == 1 and not first:
                        layer1(t - 1, L1_PARTS - 1, L1_PARTS)
                    if k == 5 and not first:
                        layer2(t - 1, 0)
                for c in range(SETS):
                    products(t, 1, c, first)
                    if not last and c > 0:
                        fill(t + 1, c - 1, first)
                    if c == 1 and not first:
                        layer2(t - 1, 1)
                    if c == 3 and not first:
                        layer3(t - 1)
                if not last:
                    fill(t + 1, SETS - 1, first)

            pe.wait_ge(consts_made, 3)
            pe.wait_ge(pads_zeroed, 1)
            pe.wait_ge(small_in, 48)
            step(0, True, False)
            pe.wait_ge(chunk_l, len(chunks))
            with pe.Fori(1, STEPS - 1) as t:
                step(t, False, False)
            step(STEPS - 1, False, True)
            layer1(STEPS - 1, 0, 1)
            for n in range(N2):
                layer2(STEPS - 1, n)
            layer3(STEPS - 1)
            pe.wait_ge(y_made, STEPS)
            nc.tensor.transpose(ps_t[0][0:2 * STEPS, 0, :], y_sb[:], ident[:]).then_inc(y_turned, 1)


def kernel(**inputs):
    import numpy as np
    import concourse.bacc as bacc
    from concourse.bass_utils import run_bass_kernel_spmd

    arrays = {name: np.ascontiguousarray(a) for name, a in inputs.items()}
    arrays["ids_oh"] = np.ascontiguousarray(arrays["ids"][:, list(OH_FIELDS)].T)
    w1 = arrays.pop("W_top1")
    pairs = NF * (NF - 1) // 2
    row = np.zeros((NF, NF), np.int64)
    a, b = np.triu_indices(NF, k=1)
    row[a, b] = row[b, a] = np.arange(pairs)
    i, j = np.nonzero(~np.eye(NF, dtype=bool))
    vec = np.array(SLOT_OF)
    laid = np.zeros((S4, SLOT, JB, H1), w1.dtype)
    laid[j // JB, i, j % JB] = w1[row[vec[i], vec[j]]]
    arrays["w1_pairs"] = laid.reshape(P, JB, H1)
    arrays["w1_dense"] = np.ascontiguousarray(w1[pairs:])
    arrays["w2"] = np.ascontiguousarray(arrays.pop("W_top2").reshape(N1, P, H2).transpose(1, 0, 2))
    arrays["w3"] = np.ascontiguousarray(arrays.pop("W_top3").reshape(N2, P).T)
    arrays["b1"] = np.ascontiguousarray(arrays.pop("b_top1").reshape(N1, P).T)
    arrays["b2"] = np.ascontiguousarray(arrays.pop("b_top2").reshape(N2, P).T)

    nc = bacc.Bacc("TRN2", target_bir_lowering=False, num_devices=1)
    ap = {name: nc.dram_tensor(name, a.shape, mybir.dt.from_np(a.dtype), kind="ExternalInput").ap()
          for name, a in arrays.items()}
    out = nc.dram_tensor("y", (B, 1), F32, kind="ExternalOutput").ap()
    tower_kernel(nc, ap["r_dense_x"], ap["ids"], ap["ids_oh"], [ap[f"tbl_{f}"] for f in GATHERED],
                 [ap[f"tbl_{f}"] for f in OH_FIELDS], ap["w1_pairs"], ap["w1_dense"],
                 ap["w2"], ap["w3"], ap["b1"], ap["b2"], out)
    return run_bass_kernel_spmd(nc, [arrays], core_ids=[0]).results[0]["y"]
```

```python
from contextlib import ExitStack

import concourse.bass as bass
from concourse import mybir

F32 = mybir.dt.float32
F32R = mybir.dt.float32r
I32 = mybir.dt.int32
ALU = mybir.AluOpType
ACT = mybir.ActivationFunctionType

B, D, F = 2048, 128, 26
NF = F + 1
H1, H2 = 512, 256
P = 128
SLOT = 32
TILE = P
PAIR = 2 * TILE
STEPS = B // PAIR
S4 = P // SLOT
GROUPS = TILE // S4
JB = 7
JS = S4 * JB
GW = 256
SETG = 4
SETS = GROUPS // SETG
N1, N2 = H1 // P, H2 // P

OH_FIELDS = (6, 7, 9, 10, 11, 12)
OH_ROWS = 1000
KT = 8
OH_P = OH_ROWS // KT
KH = KT // 2
NOH = len(OH_FIELDS)
ITEMS = [list(range(i, min(NOH, i + 2))) for i in range(0, NOH, 2)]
NI = len(ITEMS)
FILLS = [(i, k, 4 // len(tb)) for i, tb in enumerate(ITEMS) for k in range(0, KT, 4 // len(tb))]
NFILL = len(FILLS)
WEIGHT_QUADS = 4
BUFS = 3
EARLY = NI - 1
EARLY_T = ITEMS[EARLY - 1][-1] + 1
AHEAD = 8
GATHERED = tuple(f for f in range(F) if f not in OH_FIELDS)
NG = len(GATHERED)
XS = NG
OS = NG + 1
SLOT_OF = GATHERED + (F,) + OH_FIELDS
QF = 4
QUAD_SLOTS = [range(XS, XS + 1)] + [range(v, v + QF) for v in range(0, NG, QF)]
QUADS = len(QUAD_SLOTS)
assert NG % QF == 0 and QUADS % 2 == 0 and NFILL % BUFS == 0 and NFILL == 12 and AHEAD == SETS

LATE = [("quad", 0), ("quad", 1), ("fill", 8), ("quad", 2), ("fill", 9), ("fill", 10), ("quad", 3), ("fill", 11),
        ("quad", 4), ("quad", 5)]
ALL_FILLS = [("fill", h) for h in range(AHEAD)]
L1_PARTS = SETS - 1
LAST_BESIDE_QUADS = {3: (L1_PARTS, L1_PARTS + 1), 5: (L1_PARTS + 2,)}
ROWS_FROM = 5
ROWS_PARTS = 6
assert 2 * L1_PARTS - ROWS_FROM + 1 == L1_PARTS + 3


def tower_kernel(nc, x, ids, ids_oh, gathered, oh_tables, w1_pairs, w1_dense, w2, w3, b1, b2, out):
    ctx = ExitStack()
    with ctx:
        sb = lambda name, shape, dt=F32: ctx.enter_context(nc.sbuf_tensor(name, shape, dt))
        ps = lambda name, shape: ctx.enter_context(nc.psum_tensor(name, shape, F32))
        sem = lambda name: ctx.enter_context(nc.semaphore(name))

        ident = sb("ident", [P, P])
        first_row_i = sb("first_row_i", [P, 1], I32)
        first_row = sb("first_row", [P, 1])
        tab = sb("tab", [P, NOH, 2, KT, D], F32R)
        w1_sb = sb("w1_sb", [P, 2, JB + 1, H1], F32R)
        w2_sb = sb("w2_sb", [P, 2, N1, H2], F32R)
        w3_sb = sb("w3_sb", [P, N2])
        b1_sb = sb("b1_sb", [P, N1])
        b2_sb = sb("b2_sb", [P, N2])
        idx = [sb(f"idx{u}", [P, F], I32) for u in range(2)]
        rows = [sb(f"rows{u}", [P, NG + 1, D]) for u in range(2)]
        ids_b = sb("ids_b", [P, NOH, PAIR])
        onehot = [sb(f"onehot{r}", [P, 4 * PAIR], F32R) for r in range(BUFS)]
        emb = sb("emb", [P, GROUPS, 2, S4, SLOT], F32R)
        held = [sb("held0", [P, EARLY_T, TILE]),
                sb("held1", [P, NOH, TILE])]
        x_held = sb("x_held", [P, 2, S4, GROUPS], F32R)
        xz = sb("xz", [P, 2, 2, S4, GROUPS], F32R)
        gram = [sb(f"gram{u}", [P, JS, GROUPS]) for u in range(2)]
        zh = sb("zh", [P, 2, S4, JB, GROUPS], F32R)
        zl = sb("zl", [P, 2, S4, JB, GROUPS], F32R)
        h1 = sb("h1", [P, N1, PAIR])
        h1h = sb("h1h", [P, N1, PAIR], F32R)
        h1l = sb("h1l", [P, N1, PAIR], F32R)
        stage = sb("stage", [P, 512])
        h2 = h1[:, 0:N2, :]
        y_sb = sb("y_sb", [P, 2 * STEPS])
        y_rows = sb("y_rows", [2 * STEPS, TILE])
        turn = [nc.dram_tensor(f"turn{u}", (S4, SLOT, S4, JB * GROUPS), F32).ap() for u in range(2)]

        ps_t = [ps(f"ps_t{i}", [P, QF, TILE]) for i in range(2)]
        ps_g = [ps(f"ps_g{i}", [P, SETG, GW]) for i in range(2)]
        ps_m = [ps(f"ps_m{i}", [P, 2, PAIR]) for i in range(2)]

        consts_made = sem("consts_made")
        small_in = sem("small_in")
        chunk_in = [sem(f"chunk_in{r}") for r in range(10)]
        chunk_h = sem("chunk_h")
        chunk_l = sem("chunk_l")
        pads_zeroed = sem("pads_zeroed")
        room_seen = sem("room_seen")
        idx_in = [sem(f"idx_in{u}") for u in range(2)]
        ids_in = sem("ids_in")
        ids_less = sem("ids_less")
        x_in = [sem(f"x_in{u}") for u in range(2)]
        rows_in = [[sem(f"rows_in{u}_{k}") for k in range(QUADS)] for u in range(2)]
        onehot_made = sem("onehot_made")
        onehot_used = sem("onehot_used")
        item_out = sem("item_out")
        item_l = sem("item_l")
        held_h = sem("held_h")
        held_l = sem("held_l")
        quad_transposed = sem("quad_transposed")
        quad_h = sem("quad_h")
        quad_l = sem("quad_l")
        x_kept = sem("x_kept")
        set_done = sem("set_done")
        set_h = sem("set_h")
        set_moved = sem("set_moved")
        gram_out = [sem(f"gram_out{u}") for u in range(2)]
        z_in = [sem(f"z_in{u}") for u in range(2)]
        z_h = sem("z_h")
        z_l = sem("z_l")
        w1_done = sem("w1_done")
        h1_h = sem("h1_h")
        h1_l = sem("h1_l")
        w2_done = sem("w2_done")
        h2_made = sem("h2_made")
        w3_done = sem("w3_done")
        y_made = sem("y_made")
        y_turned = sem("y_turned")
        z_put = sem("z_put")
        last_zh = sem("last_zh")
        last_zl = sem("last_zl")
        rows_done = sem("rows_done")
        rows_made = sem("rows_made")
        rows_turned = sem("rows_turned")
        last_h1 = sem("last_h1")
        last_h1h = sem("last_h1h")
        last_h1l = sem("last_h1l")
        y_out = sem("y_out")

        block = ctx.enter_context(nc.Block())
        f32 = lambda ap: ap.bitcast(F32)
        x_t = x.rearrange("(t p) d -> t p d", p=TILE)
        ids_t = ids.rearrange("(t p) f -> t p f", p=TILE)
        ROWS_IN = 16 * QF
        fills_to = [max(h for h, f in enumerate(FILLS) if f[0] == i) + 1 for i in range(NI)]
        ends_item = {n - 1: i for i, n in enumerate(fills_to)}

        chunks = []
        for n in range(NOH):
            rows_of = oh_tables[n].rearrange("(p k) d -> p k d", k=KT)
            for a in range(2):
                ks = slice(KH * a, KH * (a + 1))
                chunks.append((rows_of[:, ks, :], OH_P, tab[0:OH_P, n, 0, ks, :], tab[0:OH_P, n, 1, ks, :]))
        TAB_CHUNKS = len(chunks)
        for jj in range(JB + 1):
            src = w1_pairs[:, jj, :] if jj < JB else w1_dense
            chunks.append((src, P, w1_sb[:, 0, jj, :], w1_sb[:, 1, jj, :]))
        for a in range(2):
            cs = slice(a * N1 // 2, (a + 1) * N1 // 2)
            chunks.append((w2[:, cs, :], P, w2_sb[:, 0, cs, :], w2_sb[:, 1, cs, :]))
        STAGES = [h1[:, 2 * x:2 * x + 2, :].rearrange("p a b -> p (a b)") for x in range(2)] + [stage[:]]
        NW = len(STAGES)
        STAGES += [g[:].rearrange("p j g -> p (j g)")[:, 0:512] for g in gram]
        STAGES += [rows[1][:, 4 * x:4 * x + 4, :].rearrange("p v d -> p (v d)") for x in range(NG // 4)]
        NS = len(STAGES)

        def stage_of(c):
            return c % NS if c < TAB_CHUNKS else (c - TAB_CHUNKS) % NW

        def chunks_in(c):
            before = [b for b in range(c) if stage_of(b) == stage_of(c)]
            return len(before) + 1, before[-1] + 1 if before else 0

        def staged(c):
            _, parts, hi, _ = chunks[c]
            at = STAGES[stage_of(c)][0:parts, :]
            return at if len(hi.shape) == 2 else at.rearrange("p (a b) -> p a b", a=hi.shape[1])

        def tables_beside(h):
            return range(2 * len(ITEMS[0]) * (h + 2) // 2, min(TAB_CHUNKS, 2 * len(ITEMS[0]) * (h + 3) // 2))

        def weights_beside(c):
            n, slots = len(chunks) - TAB_CHUNKS, SETS + WEIGHT_QUADS
            return range(TAB_CHUNKS + n * c // slots, TAB_CHUNKS + n * (c + 1) // slots)

        LAST = STEPS - 1
        z_last = [onehot[part][:, 0:JB * TILE].rearrange("p (j b) -> p j b", b=TILE) for part in range(2)]
        z_rows = rows[0][:, 0:JB, :].rearrange("p v d -> p (v d)")
        z_value = gram[0][:].rearrange("p j g -> p (j g)").rearrange("p (j s g) -> p j s g", j=JB, s=S4)
        MOVES = [(s, q) for s in range(S4) for q in range(S4)]
        ACT_MOVES, POOL_MOVES = 7, 2

        ROWS = [(0, range(0, N1), ps_m[0][:].rearrange("p a b -> p (a b)"), ps_t[0]),
                (1, range(0, N1 // 2), ps_g[0][:, 0, :], ps_t[1]),
                (1, range(N1 // 2, N1), ps_g[0][:, 2, :], ps_t[0])]
        h2_kept = rows[1][:, 0:4, :].rearrange("p (n a) d -> p n (a d)", n=N2)

        def put_z(engine_copy, s, q):
            engine_copy(z_value[SLOT * q:SLOT * (q + 1), :, s, :],
                        gram[1][SLOT * s:SLOT * (s + 1), JB * q:JB * (q + 1), :]).then_inc(z_put, 1)

        def last_z(u):
            return z_value if u else z_rows.rearrange("p (s j g) -> p j s g", s=S4, j=JB)

        def by_vector(part, a, b):
            return emb[:, :, part, :, a:b].rearrange("p g s f -> p f g s")

        def grouped(ap):
            return ap.rearrange("p f (g s) -> p f g s", s=S4)

        def columns(h):
            _, _, kb = FILLS[h]
            return onehot[h % BUFS][0:OH_P, :].rearrange("p (k n b) -> p k n b", k=kb, b=PAIR)

        @block.gpsimd
        def _(pool):
            nc.gpsimd.memset(ident[:], 0.0).then_inc(consts_made, 1)
            pool.wait_ge(consts_made, 1)
            nc.gpsimd.affine_select(out=ident[:], in_=ident[:], compare_op=ALU.not_equal, fill=1.0, base=0,
                                    pattern=[[-1, P]], channel_multiplier=1).then_inc(consts_made, 1)
            nc.gpsimd.iota(first_row_i[:], pattern=[[1, 1]], base=0, channel_multiplier=-KT).then_inc(consts_made, 1)

            def gather(t, first):
                for u in range(2):
                    pool.wait_ge(idx_in[u], 16 * t + 16)
                    if first and u == 1:
                        pool.wait_ge(chunk_l, TAB_CHUNKS)
                        pool.sem_inc(room_seen, 1)
                    for k in range(1, QUADS):
                        if not first:
                            pool.wait_ge(quad_transposed, 2 * QUADS * t - 2 * QUADS + QUADS * u + k + 1)
                            pool.sem_inc(room_seen, 1)
                        for v in QUAD_SLOTS[k]:
                            f = GATHERED[v]
                            pool.indirect_dma_start(
                                out=rows[u][:, v, :], out_offset=None, in_=gathered[v],
                                in_offset=bass.IndirectOffsetOnAxis(ap=idx[u][:, f:f + 1], axis=0),
                            ).then_inc(rows_in[u][k], 16)

            gather(0, True)
            with pool.Fori(1, STEPS) as t:
                gather(t, False)
            pool.wait_ge(set_moved, 2 * SETS * STEPS)
            pool.wait_ge(gram_out[0], 16 * S4 * STEPS)
            for s, q in MOVES[ACT_MOVES:ACT_MOVES + POOL_MOVES]:
                put_z(nc.gpsimd.tensor_copy, s, q)

        @block.sync
        def _(sp):
            def load_idx(t, u, first):
                if not first:
                    sp.wait_ge(rows_in[u][QUADS - 1], ROWS_IN * t)
                sp.dma_start(idx[u][:], ids_t[2 * t + u]).then_inc(idx_in[u], 16)

            def load_x(t, u, first):
                if not first:
                    sp.wait_ge(quad_transposed, 2 * QUADS * t - 2 * QUADS + QUADS * u + 1)
                sp.dma_start(rows[u][:, XS, :], x_t[2 * t + u]).then_inc(x_in[u], 16)

            def load_ids(t, first):
                if not first:
                    sp.wait_ge(onehot_made, NFILL * t)
                sp.dma_start(ids_b[:].bitcast(I32), ids_oh[:, bass.ts(t, PAIR)].partition_broadcast(P)
                             ).then_inc(ids_in, 16)

            def spread(t, u):
                sp.wait_ge(set_moved, 2 * SETS * t + SETS * (u + 1))
                for s in range(S4):
                    sp.dma_start(turn[u][:, :, s, :].rearrange("q i c -> i q c"),
                                 gram[u][SLOT * s:SLOT * (s + 1), :, :].rearrange("i (q j) g -> i q (j g)", q=S4)
                                 ).then_inc(gram_out[u], 16)

            def gather_z(t, u, first, last=False):
                if last:
                    sp.wait_ge(quad_transposed, QUADS * (2 * t + 1))
                elif not first and u == 0:
                    sp.wait_ge(w1_done, 2 * t)
                sp.wait_ge(gram_out[u], 16 * S4 * t + 16 * S4)
                sp.dma_start(z_rows if last else f32(zl[:, u]).rearrange("p s j g -> p (s j g)"),
                             turn[u].rearrange("q i s c -> (q i) (s c)")).then_inc(z_in[u], 16)

            def step(t, first, last):
                if not last:
                    load_idx(t + 1, 0, False)
                if not first:
                    spread(t - 1, 1)
                    gather_z(t - 1, 1, False)
                if not last:
                    load_x(t + 1, 0, False)
                    load_ids(t + 1, False)
                if first:
                    for c in range(TAB_CHUNKS, len(chunks)):
                        load_chunk(c)
                if not last:
                    load_idx(t + 1, 1, False)
                spread(t, 0)
                gather_z(t, 0, first, last)
                if not last:
                    load_x(t + 1, 1, False)

            def load_chunk(c):
                n, before = chunks_in(c)
                if before:
                    sp.wait_ge(chunk_l, before)
                sp.dma_start(staged(c), chunks[c][0]).then_inc(chunk_in[stage_of(c)], 16)

            load_idx(0, 0, True)
            load_chunk(0)
            load_ids(0, True)
            for c in range(1, TAB_CHUNKS):
                load_chunk(c)
                if c == 4:
                    load_idx(0, 1, True)
                    load_x(0, 0, True)
            load_x(0, 1, True)
            step(0, True, False)
            with sp.Fori(1, STEPS - 1) as t:
                step(t, False, False)
            step(STEPS - 1, False, True)
            sp.wait_ge(y_made, STEPS + 1)
            sp.dma_start(out.rearrange("(t p) o -> t (p o)", p=TILE), y_rows[:]).then_inc(y_out, 16)
            sp.wait_ge(y_out, 16)

        @block.scalar
        def _(act):
            def chunk(c):
                act.wait_ge(chunk_in[stage_of(c)], 16 * chunks_in(c)[0])
                nc.scalar.copy(chunks[c][2], staged(c)).then_inc(chunk_h, 1)

            def less(t):
                act.wait_ge(ids_in, 16 * t + 16)
                nc.scalar.activation(ids_b[:], ids_b[:].bitcast(I32), ACT.Identity,
                                     bias=first_row[:, 0:1]).then_inc(ids_less, 1)

            def item(t, i):
                act.wait_ge(onehot_used, NFILL * t + fills_to[i])
                a, n = ITEMS[i][0], len(ITEMS[i])
                nc.scalar.copy(held[1][:, a:a + n, :], ps_m[i % 2][:, 0:n, TILE:PAIR])
                src = ps_m[i % 2][:, 0:n, 0:TILE]
                if i < EARLY:
                    nc.scalar.copy(held[0][:, a:a + n, :], src).then_inc(item_out, 1)
                else:
                    nc.scalar.copy(by_vector(0, OS + a, OS + a + n), grouped(src)).then_inc(item_out, 1)

            def unhold(t, u):
                act.wait_ge(item_out, NI * t + (NI if u else EARLY))
                n = held[u].shape[1]
                nc.scalar.copy(by_vector(0, OS, OS + n), grouped(held[u][:])).then_inc(held_h, 1)

            def quad(t, u, k):
                m = QUADS * u + k
                act.wait_ge(quad_transposed, 2 * QUADS * t + m + 1)
                a, n = QUAD_SLOTS[k][0], len(QUAD_SLOTS[k])
                nc.scalar.copy(by_vector(0, a, a + n), grouped(ps_t[m % 2][:, 0:n])).then_inc(quad_h, 1)

            def move_set(t, u, c, first):
                act.wait_ge(set_done, 2 * SETS * t + SETS * u + c + 1)
                if c == 0 and not first:
                    act.wait_ge(gram_out[u], 16 * S4 * t)
                for s in range(S4):
                    ss = slice(SLOT * s, SLOT * (s + 1))
                    last = nc.scalar.activation(
                        gram[u][ss, 0:NF, SETG * c:SETG * (c + 1)].rearrange("p j g -> p g j"),
                        ps_g[c % 2][ss, :, JS * s:JS * s + NF], ACT.Copy, scale=0.5)
                last.then_inc(set_h, 1)

            def split_z(t, u):
                act.wait_ge(z_in[u], 16 * t + 16)
                nc.scalar.copy(zh[:, u], f32(zl[:, u])).then_inc(z_h, 1)

            def layer1(t, bank):
                act.wait_ge(w1_done, 2 * t + bank + 1)
                for i in range(2):
                    n = 2 * bank + i
                    for to in (h1, h1h):
                        last = nc.scalar.activation(to[:, n, :], ps_m[bank][:, i, :], ACT.Relu, bias=b1_sb[:, n:n + 1])
                    last.then_inc(h1_h, 1)

            def layer2(t, to=h2):
                act.wait_ge(w2_done, t + 1)
                for n in range(N2):
                    last = nc.scalar.activation(to[:, n, :], ps_m[1][:, n, :], ACT.Relu, bias=b2_sb[:, n:n + 1])
                last.then_inc(h2_made, 1)

            def step(t, first, last):
                if not first:
                    act.wait_ge(set_done, 2 * SETS * t)
                    act.wait_ge(x_kept, 2 * t)
                    act.wait_ge(held_l, 2 * t)
                for what, k in (ALL_FILLS if first else []) + LATE:
                    if what == "quad":
                        quad(t, 0, k)
                        if k == 1 and not first:
                            unhold(t, 0)
                    elif k in ends_item:
                        item(t, ends_item[k])
                        if first and ends_item[k] == EARLY - 1:
                            unhold(t, 0)
                if first:
                    act.wait_ge(chunk_l, TAB_CHUNKS)
                if not first:
                    split_z(t - 1, 1)
                for c in range(SETS):
                    move_set(t, 0, c, first)
                    if first:
                        for w in weights_beside(c):
                            chunk(w)
                    if c == 2 and not last:
                        less(t + 1)
                    if c == 4 and not first and not last:
                        layer1(t - 1, 0)
                act.wait_ge(x_kept, 2 * t + 1)
                for k in range(QUADS):
                    quad(t, 1, k)
                    if first and 1 <= k <= WEIGHT_QUADS:
                        for w in weights_beside(SETS + k - 1):
                            chunk(w)
                    if k == 1:
                        unhold(t, 1)
                    if k == 3 and not first:
                        layer1(t - 1, 0 if last else 1)
                for c in range(SETS):
                    move_set(t, 1, c, first)
                    if c == 2 and not first and not last:
                        layer2(t - 1)
                    if c == 3:
                        if last:
                            split_last_z(0)
                        else:
                            split_z(t, 0)
                    if last and c == ROWS_FROM:
                        layer1(t - 1, 1)
                    if not last and c == fills_to[0] + 1:
                        act.wait_ge(held_l, 2 * t + 2)
                        item(t + 1, 0)
                if not last:
                    item(t + 1, EARLY - 1)

            def split_last_z(u):
                if u == 0:
                    act.wait_ge(z_in[0], 16 * STEPS)
                    act.wait_ge(onehot_used, NFILL * STEPS)
                else:
                    act.wait_ge(set_moved, 2 * SETS * STEPS)
                    act.wait_ge(gram_out[0], 16 * S4 * STEPS)
                    for s, q in MOVES[:ACT_MOVES]:
                        put_z(nc.scalar.copy, s, q)
                    act.wait_ge(rows_done, 1)
                    act.wait_ge(z_put, len(MOVES))
                for js in (slice(0, JB // 2), slice(JB // 2, JB)):
                    nc.scalar.copy(z_last[0][:, js, :].rearrange("p j (s g) -> p j s g", s=S4),
                                   last_z(u)[:, js]).then_inc(last_zh, 1)

            def keep_rows(r):
                _, ns, src, _ = ROWS[r]
                if r:
                    act.wait_ge(rows_turned, 1)
                act.wait_ge(rows_done, r + 1)
                nc.scalar.copy(stage[:, P * ns[0]:P * (ns[-1] + 1)], src).then_inc(rows_made, 1)

            def last_layer1(r):
                u, ns, _, src = ROWS[r]
                if r == 0:
                    act.wait_ge(w2_done, LAST)
                act.wait_ge(rows_turned, r + 1)
                for i, n in enumerate(ns):
                    nc.scalar.activation(h1[:, n, TILE * u:TILE * (u + 1)], src[:, i, :], ACT.Relu,
                                         bias=b1_sb[:, n:n + 1]).then_inc(last_h1, 1)

            for dst, src in ((b1_sb, b1), (b2_sb, b2), (w3_sb, w3)):
                act.dma_start(dst[:], src).then_inc(small_in, 16)
            act.wait_ge(consts_made, 4)
            chunk(0)
            less(0)
            for c in range(1, TAB_CHUNKS):
                chunk(c)
            act.wait_ge(small_in, 48)
            step(0, True, False)
            with act.Fori(1, STEPS - 1) as t:
                step(t, False, False)
            step(STEPS - 1, False, True)
            split_last_z(1)
            layer2(STEPS - 2, h2_kept)
            for r in range(len(ROWS)):
                keep_rows(r)
                last_layer1(r)
            act.wait_ge(w2_done, STEPS)
            for n in range(N2):
                last = nc.scalar.activation(h2[:, n, :], ps_m[n][:, 0, :], ACT.Relu, bias=b2_sb[:, n:n + 1])
            last.then_inc(h2_made, 1)

        @block.vector
        def _(dve):
            def chunk(c):
                dve.wait_ge(chunk_h, c + 1)
                _, _, hi, lo = chunks[c]
                nc.vector.tensor_tensor(lo, staged(c), f32(hi), ALU.subtract).then_inc(chunk_l, 1)

            def fill(t, h, first):
                i, k0, kb = FILLS[h]
                if h == 0:
                    dve.wait_ge(ids_less, t + 1)
                if h >= BUFS or not first:
                    dve.wait_ge(onehot_used, NFILL * t + h - BUFS + 1)
                for k in range(kb):
                    a, n = ITEMS[i][0], len(ITEMS[i])
                    last = nc.vector.tensor_scalar(columns(h)[:, k], ids_b[0:OH_P, a:a + n, :], float(k0 + k), None,
                                                   ALU.is_equal)
                last.then_inc(onehot_made, 1)

            def item(t, i):
                dve.wait_ge(item_out, NI * t + i + 1)
                a, n = OS + ITEMS[i][0], OS + ITEMS[i][-1] + 1
                nc.vector.tensor_tensor(by_vector(1, a, n), grouped(ps_m[i % 2][:, 0:n - a, 0:TILE]),
                                        f32(by_vector(0, a, n)), ALU.subtract).then_inc(item_l, 1)

            def unhold(t, u):
                dve.wait_ge(held_h, 2 * t + u + 1)
                n = held[u].shape[1]
                nc.vector.tensor_tensor(by_vector(1, OS, OS + n), grouped(held[u][:]), f32(by_vector(0, OS, OS + n)),
                                        ALU.subtract).then_inc(held_l, 1)

            def quad(t, u, k):
                m = QUADS * u + k
                a, n = QUAD_SLOTS[k][0], QUAD_SLOTS[k][-1] + 1
                dve.wait_ge(quad_h, 2 * QUADS * t + m + 1)
                nc.vector.tensor_tensor(by_vector(1, a, n), grouped(ps_t[m % 2][:, 0:n - a]), f32(by_vector(0, a, n)),
                                        ALU.subtract).then_inc(quad_l, 1)

            def keep_x(t, u):
                dve.wait_ge(quad_l, 2 * QUADS * t + QUADS * u + 1)
                to = xz[:, :, 1] if u else x_held[:]
                nc.vector.tensor_copy(to.rearrange("p h s g -> p g h s"), f32(emb[:, :, :, :, XS])).then_inc(x_kept, 1)

            def unhold_x(t, first):
                if not first:
                    dve.wait_ge(w1_done, 2 * t)
                dve.wait_ge(x_kept, 2 * t + 1)
                nc.vector.tensor_copy(xz[:, :, 0], f32(x_held[:]))

            def move_set(t, u, c):
                dve.wait_ge(set_h, 2 * SETS * t + SETS * u + c + 1)
                for s in range(S4):
                    ss = slice(SLOT * s, SLOT * (s + 1))
                    to = gram[u][ss, 0:NF, SETG * c:SETG * (c + 1)].rearrange("p j g -> p g j")
                    last = nc.vector.tensor_tensor(to, ps_g[c % 2][ss, :, JS * (S4 + s):JS * (S4 + s) + NF], to, ALU.add)
                last.then_inc(set_moved, 1)

            def split_z(t, u):
                dve.wait_ge(z_h, 2 * t + u + 1)
                nc.vector.tensor_tensor(zl[:, u], f32(zl[:, u]), f32(zh[:, u]), ALU.subtract).then_inc(z_l, 1)

            def layer1(t, bank):
                for n in range(2 * bank, 2 * bank + 2):
                    dve.wait_ge(h1_h, N1 * t + n + 1)
                    nc.vector.tensor_tensor(h1l[:, n, :], h1[:, n, :], f32(h1h[:, n, :]), ALU.subtract).then_inc(h1_l, 1)

            def keep_y(t):
                dve.wait_ge(w3_done, t + 1)
                nc.vector.tensor_copy(y_sb[:, bass.ts(t, 2)], ps_m[1][:, 0, 0:2]).then_inc(y_made, 1)

            def step(t, first, last):
                if first:
                    for h in range(BUFS):
                        fill(t, h, True)
                else:
                    fill(t, NFILL - 2, False)
                for what, k in (ALL_FILLS if first else []) + LATE:
                    if what == "quad":
                        quad(t, 0, k)
                        if k == 1 and not first:
                            unhold(t, 0)
                        continue
                    if k + BUFS < NFILL:
                        fill(t, k + BUFS, first)
                    if k in ends_item and k >= AHEAD:
                        item(t, ends_item[k])
                    if first and k == fills_to[EARLY - 1] - 1:
                        unhold(t, 0)
                    if first:
                        for c in tables_beside(k):
                            chunk(c)
                keep_x(t, 0)
                if first:
                    for u in range(2):
                        nc.vector.memset(gram[u][:, NF:JS, :], 0.0)
                if not first:
                    split_z(t - 1, 1)
                for c in range(SETS):
                    move_set(t, 0, c)
                    if first:
                        for w in weights_beside(c):
                            chunk(w)
                    if c == 4 and not first and not last:
                        layer1(t - 1, 0)
                    if c in (3, 4, 5) and not last:
                        fill(t + 1, c - 3, False)
                for k in range(QUADS):
                    quad(t, 1, k)
                    if first and 1 <= k <= WEIGHT_QUADS:
                        for w in weights_beside(SETS + k - 1):
                            chunk(w)
                    if k == 1:
                        unhold(t, 1)
                    if k == 3 and not first:
                        layer1(t - 1, 0 if last else 1)
                if not last:
                    unhold_x(t, first)
                    keep_x(t, 1)
                for c in range(SETS):
                    move_set(t, 1, c)
                    if not last and c > 0:
                        fill(t + 1, c + BUFS - 1, False)
                    if c == 3 and not first and not last:
                        keep_y(t - 1)
                    if c == 3:
                        if last:
                            split_last_z(0)
                        else:
                            split_z(t, 0)
                    if last and c == ROWS_FROM:
                        unhold_x(t, False)
                        keep_x(t, 1)
                        layer1(t - 1, 1)

            def split_last_z(u):
                if u:
                    dve.wait_ge(set_moved, 2 * SETS * STEPS)
                    dve.wait_ge(gram_out[0], 16 * S4 * STEPS)
                    for s, q in MOVES[ACT_MOVES + POOL_MOVES:]:
                        put_z(nc.vector.tensor_copy, s, q)
                dve.wait_ge(last_zh, 2 * u + 2)
                nc.vector.tensor_tensor(z_last[1].rearrange("p j (s g) -> p j s g", s=S4), last_z(u),
                                        f32(z_last[0]).rearrange("p j (s g) -> p j s g", s=S4), ALU.subtract
                                        ).then_inc(last_zl, 1)

            def last_layer1(u, ns):
                cs = slice(TILE * u, TILE * (u + 1))
                if u == 0:
                    dve.wait_ge(w2_done, LAST)
                for n in ns:
                    dve.wait_ge(last_h1, N1 * u + n + 1)
                    nc.vector.tensor_copy(h1h[:, n, cs], h1[:, n, cs]).then_inc(last_h1h, 1)
                    dve.wait_ge(last_h1h, N1 * u + n + 1)
                    nc.vector.tensor_tensor(h1l[:, n, cs], h1[:, n, cs], f32(h1h[:, n, cs]), ALU.subtract
                                            ).then_inc(last_h1l, 1)

            nc.vector.memset(f32(emb[:, :, :, :, NF:SLOT].rearrange("p g h s f -> p (g h s) f")), 0.0
                             ).then_inc(pads_zeroed, 1)
            dve.wait_ge(consts_made, 3)
            nc.vector.tensor_copy(first_row[:], first_row_i[:]).then_inc(consts_made, 1)
            for c in range(2 * len(ITEMS[0])):
                chunk(c)
            step(0, True, False)
            with dve.Fori(1, STEPS - 1) as t:
                step(t, False, False)
            step(STEPS - 1, False, True)
            split_last_z(1)
            last_layer1(0, range(N1))
            last_layer1(1, ROWS[1][1])
            keep_y(STEPS - 2)
            last_layer1(1, ROWS[2][1])
            keep_y(STEPS - 1)
            dve.wait_ge(y_turned, 1)
            nc.vector.tensor_copy(y_rows[:].rearrange("t (g s) -> t s g", s=S4),
                                  ps_t[0][0:2 * STEPS, 0, :].rearrange("t (s g) -> t s g", s=S4)).then_inc(y_made, 1)

        @block.tensor
        def _(pe):
            def fill(t, h, first):
                i, k0, kb = FILLS[h]
                if i == 1 and h == fills_to[0] and not first:
                    pe.wait_ge(y_made, t - 1)
                if i >= 2 and h == fills_to[i - 1]:
                    pe.wait_ge(item_out, NI * t + i - 1)
                pe.wait_ge(onehot_made, NFILL * t + h + 1)
                for k in range(kb):
                    for n, tb in enumerate(ITEMS[i]):
                        for part in range(2):
                            last = nc.tensor.matmul(ps_m[i % 2][:, n, :], tab[0:OH_P, tb, part, k0 + k, :],
                                                    columns(h)[:, k, n, :], start=(k0, k, n, part) == (0, 0, 0, 0),
                                                    stop=(k0 + k, n, part) == (KT - 1, len(ITEMS[i]) - 1, 1),
                                                    skip_group_check=True)
                last.then_inc(onehot_used, 1)

            def quad(t, u, k, first):
                m = QUADS * u + k
                if m >= 2 or not first:
                    pe.wait_ge(quad_l, 2 * QUADS * t + m - 1)
                if k == 0:
                    pe.wait_ge(x_in[u], 16 * t + 16)
                else:
                    pe.wait_ge(rows_in[u][k], ROWS_IN * t + ROWS_IN)
                for i, v in enumerate(QUAD_SLOTS[k]):
                    last = nc.tensor.transpose(ps_t[m % 2][:, i, :], rows[u][:, v, :], ident[:])
                last.then_inc(quad_transposed, 1)

            def products(t, u, c, first):
                if c == 0:
                    pe.wait_ge(quad_l, 2 * QUADS * t + QUADS * (u + 1))
                    pe.wait_ge(held_l, 2 * t + u + 1)
                    if u == 0:
                        pe.wait_ge(item_l, (NI - EARLY) * t + NI - EARLY)
                if c >= 2 or u == 1 or not first:
                    pe.wait_ge(set_moved, 2 * SETS * t + SETS * u + c - 1)
                for i in range(SETG):
                    g = SETG * c + i
                    last = nc.tensor.matmul(ps_g[c % 2][:, i, 0:2 * S4 * JS],
                                            emb[:, g, 0].rearrange("p s f -> p (s f)"),
                                            emb[:, g, :, :, 0:JS].rearrange("p h s f -> p (h s) f"),
                                            start=True, stop=True)
                last.then_inc(set_done, 1)

            def terms(w, blocks, n):
                cols = slice(P * n, P * (n + 1))
                return [(w[:, wp, b, cols], v[vp]) for wp, vp in ((0, 0), (0, 1), (1, 0)) for b, v in enumerate(blocks)]

            z_blocks = [[v[:, :, :, jj, :].rearrange("p u s g -> p (u s) g") for v in (zh, zl)] for jj in range(JB)]
            z_blocks.append([xz[:, h].rearrange("p u s g -> p (u s g)") for h in range(2)])
            L1 = [(n, i, *lr) for n in range(N1) for i, lr in enumerate(terms(w1_sb, z_blocks, n))]
            per_block = len(L1) // N1

            def layer1(t, part, parts):
                if part == 0:
                    pe.wait_ge(z_l, 2 * t + 2)
                    pe.wait_ge(x_kept, 2 * t + 2)
                for n, i, lhs, rhs in L1[part * len(L1) // parts:(part + 1) * len(L1) // parts]:
                    last = nc.tensor.matmul(ps_m[n // 2][:, n % 2, :], lhs, rhs, start=i == 0, stop=i == per_block - 1)
                    if n % 2 and i == per_block - 1:
                        last.then_inc(w1_done, 1)

            def rows_layer1(r, part, parts):
                u, ns, to, _ = ROWS[r]
                cols = slice(P * ns[0], P * (ns[-1] + 1))
                z = [[z_last[vp][:, jj, :] for vp in range(2)] for jj in range(JB)]
                z.append([xz[:, vp, u].rearrange("p s g -> p (s g)") for vp in range(2)])
                tt = [(v[vp], w1_sb[:, wp, b, cols], vp) for wp, vp in ((0, 0), (1, 0), (0, 1)) for b, v in enumerate(z)]
                if part == 0:
                    if r == 0:
                        pe.wait_ge(h1_l, N1 * LAST - N1 + 2)
                    else:
                        pe.wait_ge(set_moved, 2 * SETS * STEPS)
                for i in range(part * len(tt) // parts, (part + 1) * len(tt) // parts):
                    lhs, rhs, vp = tt[i]
                    if i == JB:
                        pe.wait_ge(x_kept, 2 * STEPS)
                    if i in (0, JB // 2):
                        pe.wait_ge(last_zh, 2 * u + (2 if i else 1))
                    if vp and not tt[i - 1][2]:
                        pe.wait_ge(last_zl, u + 1)
                    last = nc.tensor.matmul(to, lhs, rhs, start=i == 0, stop=i == len(tt) - 1)
                if part == parts - 1:
                    last.then_inc(rows_done, 1)

            def turn_rows(r):
                _, ns, _, to = ROWS[r]
                if r == 2:
                    pe.wait_ge(last_h1, N1)
                pe.wait_ge(rows_made, r + 1)
                for i, n in enumerate(ns):
                    last = nc.tensor.transpose(to[:, i, :], stage[:, P * n:P * (n + 1)], ident[:])
                last.then_inc(rows_turned, 1)

            def last_layer2():
                for c in range(N1):
                    pe.wait_ge(last_h1l, N1 + c + 1)
                    for n in range(N2):
                        if c == 0 and n == 1:
                            pe.wait_ge(y_made, LAST)
                        cols = slice(P * n, P * (n + 1))
                        for i, (w, v) in enumerate(((0, h1h), (0, h1l), (1, h1h))):
                            last = nc.tensor.matmul(ps_m[n][:, 0, :], w2_sb[:, w, c, cols], v[:, c, :],
                                                    start=(c, i) == (0, 0), stop=(c, i) == (N1 - 1, 2))
                last.then_inc(w2_done, 1)

            def layer2(t, n):
                if n == 0:
                    pe.wait_ge(h1_l, N1 * t + N1)
                tt = terms(w2_sb, [(h1h[:, c, :], h1l[:, c, :]) for c in range(N1)], n)
                for i, (lhs, rhs) in enumerate(tt):
                    last = nc.tensor.matmul(ps_m[1][:, n, :], lhs, rhs, start=i == 0, stop=i == len(tt) - 1)
                if n == N2 - 1:
                    last.then_inc(w2_done, 1)

            def layer3(t, values=h2):
                pe.wait_ge(h2_made, t + 1)
                for u in range(2):
                    for n in range(N2):
                        last = nc.tensor.matmul(ps_m[1][:, 0, u:u + 1], values[:, n, TILE * u:TILE * (u + 1)],
                                                w3_sb[:, n:n + 1], start=n == 0, stop=n == N2 - 1)
                last.then_inc(w3_done, 1)

            def step(t, first, last):
                parts = 2 * L1_PARTS if last else L1_PARTS
                for what, k in (ALL_FILLS if first else []) + LATE:
                    if what == "quad":
                        quad(t, 0, k, first)
                    elif what == "fill":
                        if first and FILLS[k][1] == 0:
                            pe.wait_ge(chunk_l, 2 * ITEMS[FILLS[k][0]][-1] + 2)
                        fill(t, k, True)
                for c in range(SETS):
                    if 2 <= c and not first:
                        layer1(t - 1, c - 2, parts)
                    products(t, 0, c, first)
                for k in range(QUADS):
                    quad(t, 1, k, first)
                    if k == 1 and not first:
                        layer1(t - 1, L1_PARTS - 1, parts)
                    if last:
                        for part in LAST_BESIDE_QUADS.get(k, ()):
                            layer1(t - 1, part, parts)
                    if k == 5 and not first and not last:
                        layer2(t - 1, 0)
                for c in range(SETS):
                    products(t, 1, c, first)
                    if not last and c > 0:
                        fill(t + 1, c - 1, first)
                    if c == 1 and not first and not last:
                        layer2(t - 1, 1)
                    if c == 3 and not first and not last:
                        layer3(t - 1)
                    if last and 1 <= c < ROWS_FROM:
                        layer1(t - 1, parts - ROWS_FROM + c, parts)
                    if last and c >= ROWS_FROM:
                        rows_layer1(0, c - ROWS_FROM, ROWS_PARTS)
                if not last:
                    fill(t + 1, SETS - 1, first)

            pe.wait_ge(consts_made, 3)
            pe.wait_ge(pads_zeroed, 1)
            pe.wait_ge(small_in, 48)
            step(0, True, False)
            pe.wait_ge(chunk_l, len(chunks))
            with pe.Fori(1, STEPS - 1) as t:
                step(t, False, False)
            step(STEPS - 1, False, True)
            for part in range(SETS - ROWS_FROM, ROWS_PARTS):
                rows_layer1(0, part, ROWS_PARTS)
            for n in range(N2):
                layer2(STEPS - 2, n)
            for r in (1, 2):
                rows_layer1(r, 0, 2)
                turn_rows(r - 1)
                rows_layer1(r, 1, 2)
            layer3(STEPS - 2, h2_kept)
            turn_rows(2)
            last_layer2()
            layer3(STEPS - 1)
            pe.wait_ge(y_made, STEPS)
            nc.tensor.transpose(ps_t[0][0:2 * STEPS, 0, :], y_sb[:], ident[:]).then_inc(y_turned, 1)


def kernel(**inputs):
    import numpy as np
    import concourse.bacc as bacc
    from concourse.bass_utils import run_bass_kernel_spmd

    arrays = {name: np.ascontiguousarray(a) for name, a in inputs.items()}
    arrays["ids_oh"] = np.ascontiguousarray(arrays["ids"][:, list(OH_FIELDS)].T)
    w1 = arrays.pop("W_top1")
    pairs = NF * (NF - 1) // 2
    row = np.zeros((NF, NF), np.int64)
    a, b = np.triu_indices(NF, k=1)
    row[a, b] = row[b, a] = np.arange(pairs)
    i, j = np.nonzero(~np.eye(NF, dtype=bool))
    vec = np.array(SLOT_OF)
    laid = np.zeros((S4, SLOT, JB, H1), w1.dtype)
    laid[j // JB, i, j % JB] = w1[row[vec[i], vec[j]]]
    arrays["w1_pairs"] = laid.reshape(P, JB, H1)
    arrays["w1_dense"] = np.ascontiguousarray(w1[pairs:])
    arrays["w2"] = np.ascontiguousarray(arrays.pop("W_top2").reshape(N1, P, H2).transpose(1, 0, 2))
    arrays["w3"] = np.ascontiguousarray(arrays.pop("W_top3").reshape(N2, P).T)
    arrays["b1"] = np.ascontiguousarray(arrays.pop("b_top1").reshape(N1, P).T)
    arrays["b2"] = np.ascontiguousarray(arrays.pop("b_top2").reshape(N2, P).T)

    nc = bacc.Bacc("TRN2", target_bir_lowering=False, num_devices=1)
    ap = {name: nc.dram_tensor(name, a.shape, mybir.dt.from_np(a.dtype), kind="ExternalInput").ap()
          for name, a in arrays.items()}
    out = nc.dram_tensor("y", (B, 1), F32, kind="ExternalOutput").ap()
    tower_kernel(nc, ap["r_dense_x"], ap["ids"], ap["ids_oh"], [ap[f"tbl_{f}"] for f in GATHERED],
                 [ap[f"tbl_{f}"] for f in OH_FIELDS], ap["w1_pairs"], ap["w1_dense"],
                 ap["w2"], ap["w3"], ap["b1"], ap["b2"], out)
    return run_bass_kernel_spmd(nc, [arrays], core_ids=[0]).results[0]["y"]
```
